# Optimizing a Trainium2 kernel written in Bass

```python
import numpy as np
import jax
import jax.numpy as jnp

def _softmax(x, axis=-1):
    return jax.nn.softmax(x, axis=axis)

def _gelu(x):
    return jax.nn.gelu(x, approximate=True)

def _silu(x):
    return jax.nn.silu(x)

def _sigmoid(x):
    return jax.nn.sigmoid(x)

def _layernorm(x, axis=-1, eps=1e-05):
    m = jnp.mean(x, axis=axis, keepdims=True)
    v = jnp.var(x, axis=axis, keepdims=True)
    return (x - m) / jnp.sqrt(v + eps)

def _scatter_add(tgt, idx, src, axis=0):
    return tgt.at[idx].add(src)

def _segment_sum(src, seg, n):
    return jax.ops.segment_sum(src, seg, n)
kernel_name = 'mk_sandwich_d1_jaxref_r8_531cce'

def setup_inputs(seed: int=0):
    np.random.seed(seed)
    _w = jnp.asarray

    def _L0_attn_setup():
        import jax, jax.numpy as jnp
        import numpy as np
        import math
        B, S, E = (2, 256, 128)
        H, DC, DR = (16, 32, 128)
        HD = E // H

        def _linear_params(key, din, dout):
            k1, k2 = jax.random.split(key)
            bound = 1.0 / math.sqrt(din)
            w = jax.random.uniform(k1, (din, dout), minval=-bound, maxval=bound, dtype=jnp.float32)
            b = jax.random.uniform(k2, (dout,), minval=-bound, maxval=bound, dtype=jnp.float32)
            return (w, b)

        def _gelu(x):
            return jax.nn.gelu(x, approximate=False)

        def _rope_cos_sin(seq_len, d_rope):
            inv_freq = 1.0 / 10000.0 ** (jnp.arange(0, d_rope, 2, dtype=jnp.float32) / d_rope)
            t = jnp.arange(seq_len, dtype=jnp.float32)
            freqs = t[:, None] * inv_freq[None, :]
            emb = jnp.concatenate([freqs, freqs], axis=-1)
            return (jnp.cos(emb), jnp.sin(emb))

        def _apply_rope(x, cos, sin):
            d = x.shape[-1]
            x1, x2 = (x[..., :d // 2], x[..., d // 2:])
            rot = jnp.concatenate([-x2, x1], axis=-1)
            return x * cos + rot * sin
        key = jax.random.key(seed)
        ks = jax.random.split(key, 10)
        x = jax.random.normal(ks[0], (B, S, E), dtype=jnp.float32)
        wq, bq = _linear_params(ks[1], E, DC)
        wqc, bqc = _linear_params(ks[2], DC, E - DR)
        wqr, bqr = _linear_params(ks[3], E, DR)
        wkv, bkv = _linear_params(ks[4], E, DC)
        wkr, bkr = _linear_params(ks[5], E, DR)
        wkc, bkc = _linear_params(ks[6], DC, E - DR)
        wv, bv = _linear_params(ks[7], DC, E)
        wo, bo = _linear_params(ks[8], E, E)
        return dict(x=x, wq=wq, bq=bq, wqc=wqc, bqc=bqc, wqr=wqr, bqr=bqr, wkv=wkv, bkv=bkv, wkr=wkr, bkr=bkr, wkc=wkc, bkc=bkc, wv=wv, bv=bv, wo=wo, bo=bo)
    _L0_attn_in = _L0_attn_setup()

    def _L0_ffn_setup():
        import jax, jax.numpy as jnp
        import numpy as np
        EPS = 1e-05
        LN_EPS = 1e-05
        NUM_EXPERTS = 8
        TOP_K = 2
        HIDDEN = 128
        INTER = 256

        def _swiglu(x, wg, wu, wd):
            return jax.nn.silu(x @ wg) * (x @ wu) @ wd
        key = jax.random.key(seed)
        ks = jax.random.split(key, 10)
        B, S, H, I, E = (8, 512, HIDDEN, INTER, NUM_EXPERTS)
        std_h = 1.0 / np.sqrt(H)
        std_i = 1.0 / np.sqrt(I)
        return {'x': jax.random.normal(ks[0], (B, S, H), dtype=jnp.float32), 'ln_scale': jnp.ones((H,), dtype=jnp.float32), 'ln_bias': jnp.zeros((H,), dtype=jnp.float32), 'gate_w': jax.random.normal(ks[1], (E, H), dtype=jnp.float32) * 0.01, 'Wg': jax.random.normal(ks[2], (E, H, I), dtype=jnp.float32) * std_h, 'Wu': jax.random.normal(ks[3], (E, H, I), dtype=jnp.float32) * std_h, 'Wd': jax.random.normal(ks[4], (E, I, H), dtype=jnp.float32) * std_i, 'sWg': jax.random.normal(ks[5], (H, I), dtype=jnp.float32) * std_h, 'sWu': jax.random.normal(ks[6], (H, I), dtype=jnp.float32) * std_h, 'sWd': jax.random.normal(ks[7], (I, H), dtype=jnp.float32) * std_i}
    _L0_ffn_in = _L0_ffn_setup()
    _d = {'L0_attn_x': _L0_attn_in['x'], 'L0_attn_wq': _L0_attn_in['wq'], 'L0_attn_bq': _L0_attn_in['bq'], 'L0_attn_wqc': _L0_attn_in['wqc'], 'L0_attn_bqc': _L0_attn_in['bqc'], 'L0_attn_wqr': _L0_attn_in['wqr'], 'L0_attn_bqr': _L0_attn_in['bqr'], 'L0_attn_wkv': _L0_attn_in['wkv'], 'L0_attn_bkv': _L0_attn_in['bkv'], 'L0_attn_wkr': _L0_attn_in['wkr'], 'L0_attn_bkr': _L0_attn_in['bkr'], 'L0_attn_wkc': _L0_attn_in['wkc'], 'L0_attn_bkc': _L0_attn_in['bkc'], 'L0_attn_wv': _L0_attn_in['wv'], 'L0_attn_bv': _L0_attn_in['bv'], 'L0_attn_wo': _L0_attn_in['wo'], 'L0_attn_bo': _L0_attn_in['bo'], 'L0_ffn_ln_scale': _L0_ffn_in['ln_scale'], 'L0_ffn_ln_bias': _L0_ffn_in['ln_bias'], 'L0_ffn_gate_w': _L0_ffn_in['gate_w'], 'L0_ffn_Wg': _L0_ffn_in['Wg'], 'L0_ffn_Wu': _L0_ffn_in['Wu'], 'L0_ffn_Wd': _L0_ffn_in['Wd'], 'L0_ffn_sWg': _L0_ffn_in['sWg'], 'L0_ffn_sWu': _L0_ffn_in['sWu'], 'L0_ffn_sWd': _L0_ffn_in['sWd']}
    _x0 = _d['L0_attn_x']
    _d['L0_attn_x'] = jax.random.normal(jax.random.fold_in(jax.random.key(seed), 1), (4, 1024, 128), dtype=_x0.dtype)
    del _x0
    return _d

def reference(L0_attn_x, L0_attn_wq, L0_attn_bq, L0_attn_wqc, L0_attn_bqc, L0_attn_wqr, L0_attn_bqr, L0_attn_wkv, L0_attn_bkv, L0_attn_wkr, L0_attn_bkr, L0_attn_wkc, L0_attn_bkc, L0_attn_wv, L0_attn_bv, L0_attn_wo, L0_attn_bo, L0_ffn_ln_scale, L0_ffn_ln_bias, L0_ffn_gate_w, L0_ffn_Wg, L0_ffn_Wu, L0_ffn_Wd, L0_ffn_sWg, L0_ffn_sWu, L0_ffn_sWd):

    def _L0_attn_ref(x, wq, bq, wqc, bqc, wqr, bqr, wkv, bkv, wkr, bkr, wkc, bkc, wv, bv, wo, bo):
        import jax, jax.numpy as jnp
        import numpy as np
        import math
        B, S, E = (2, 256, 128)
        H, DC, DR = (16, 32, 128)
        HD = E // H

        def _linear_params(key, din, dout):
            k1, k2 = jax.random.split(key)
            bound = 1.0 / math.sqrt(din)
            w = jax.random.uniform(k1, (din, dout), minval=-bound, maxval=bound, dtype=jnp.float32)
            b = jax.random.uniform(k2, (dout,), minval=-bound, maxval=bound, dtype=jnp.float32)
            return (w, b)

        def _gelu(x):
            return jax.nn.gelu(x, approximate=False)

        def _rope_cos_sin(seq_len, d_rope):
            inv_freq = 1.0 / 10000.0 ** (jnp.arange(0, d_rope, 2, dtype=jnp.float32) / d_rope)
            t = jnp.arange(seq_len, dtype=jnp.float32)
            freqs = t[:, None] * inv_freq[None, :]
            emb = jnp.concatenate([freqs, freqs], axis=-1)
            return (jnp.cos(emb), jnp.sin(emb))

        def _apply_rope(x, cos, sin):
            d = x.shape[-1]
            x1, x2 = (x[..., :d // 2], x[..., d // 2:])
            rot = jnp.concatenate([-x2, x1], axis=-1)
            return x * cos + rot * sin
        b, s, _ = x.shape
        cq = _gelu(x @ wq + bq)
        q_c = cq @ wqc + bqc
        q_r = x @ wqr + bqr
        ckv = _gelu(x @ wkv + bkv)
        k_r = x @ wkr + bkr
        k_c = ckv @ wkc + bkc
        v = (ckv @ wv + bv).reshape(b, s, H, HD).transpose(0, 2, 1, 3)
        cos, sin = _rope_cos_sin(s, DR)
        q_r = _apply_rope(q_r, cos, sin)
        k_r = _apply_rope(k_r, cos, sin)
        q = _gelu(jnp.concatenate([q_c, q_r], axis=-1)).reshape(b, s, H, HD).transpose(0, 2, 1, 3)
        k = _gelu(jnp.concatenate([k_c, k_r], axis=-1)).reshape(b, s, H, HD).transpose(0, 2, 1, 3)
        scale = 1.0 / math.sqrt(HD)
        scores = jnp.einsum('bhqd,bhkd->bhqk', q, k) * scale
        causal = jnp.triu(jnp.ones((s, s), dtype=bool), k=1)
        scores = jnp.where(causal[None, None], -jnp.inf, scores)
        attn = jax.nn.softmax(scores, axis=-1)
        out = jnp.einsum('bhqk,bhkd->bhqd', attn, v)
        out = out.transpose(0, 2, 1, 3).reshape(b, s, E)
        return out @ wo + bo

    def _L0_ffn_ref(x, ln_scale, ln_bias, gate_w, Wg, Wu, Wd, sWg, sWu, sWd):
        import jax, jax.numpy as jnp
        import numpy as np
        EPS = 1e-05
        LN_EPS = 1e-05
        NUM_EXPERTS = 8
        TOP_K = 2
        HIDDEN = 128
        INTER = 256

        def _swiglu(x, wg, wu, wd):
            return jax.nn.silu(x @ wg) * (x @ wu) @ wd
        B, S, H = x.shape
        xf = x.reshape(-1, H)
        mu = jnp.mean(xf, axis=-1, keepdims=True)
        var = jnp.var(xf, axis=-1, keepdims=True)
        xn = (xf - mu) * jax.lax.rsqrt(var + LN_EPS) * ln_scale + ln_bias
        logits = xn @ gate_w.T
        probs = jax.nn.softmax(logits, axis=-1)
        tk_probs, tk_idx = jax.lax.top_k(probs, TOP_K)
        tk_probs = tk_probs / (jnp.sum(tk_probs, axis=-1, keepdims=True) + EPS)
        onehot = tk_idx[..., None] == jnp.arange(NUM_EXPERTS)[None, None, :]
        w = jnp.sum(tk_probs[..., None] * onehot.astype(tk_probs.dtype), axis=1)
        out = _swiglu(xf, sWg, sWu, sWd)
        for e in range(NUM_EXPERTS):
            out = out + w[:, e:e + 1] * _swiglu(xf, Wg[e], Wu[e], Wd[e])
        return out.reshape(B, S, H)
    x = L0_attn_x
    x = x + _layernorm(_L0_attn_ref(_layernorm(x, axis=-1), L0_attn_wq, L0_attn_bq, L0_attn_wqc, L0_attn_bqc, L0_attn_wqr, L0_attn_bqr, L0_attn_wkv, L0_attn_bkv, L0_attn_wkr, L0_attn_bkr, L0_attn_wkc, L0_attn_bkc, L0_attn_wv, L0_attn_bv, L0_attn_wo, L0_attn_bo), axis=-1)
    x = x + _layernorm(_L0_ffn_ref(_layernorm(x, axis=-1), L0_ffn_ln_scale, L0_ffn_ln_bias, L0_ffn_gate_w, L0_ffn_Wg, L0_ffn_Wu, L0_ffn_Wd, L0_ffn_sWg, L0_ffn_sWu, L0_ffn_sWd), axis=-1)
    return x

_drawn_inputs = setup_inputs


def setup_inputs(seed=0):
    import zlib

    import numpy as np

    out = dict(_drawn_inputs(seed))
    spreads = {'L0_ffn_ln_scale': (1.0, 0.2), 'L0_ffn_ln_bias': (0.0, 0.1)}
    factors = {'L0_attn_bqr': 14.865, 'L0_attn_bkr': 19.197}
    for name, (base, spread) in spreads.items():
        noise = np.random.default_rng([zlib.crc32(name.encode()), seed]).standard_normal(out[name].shape)
        drawn = base * np.exp(spread * noise) if base else spread * noise
        out[name] = jnp.asarray(drawn.astype(out[name].dtype))
    for name, factor in factors.items():
        out[name] = (out[name] * factor).astype(out[name].dtype)
    return out
```

```python
from contextlib import ExitStack

import numpy as np

import concourse.bass as bass
from concourse import mybir

F32 = mybir.dt.float32
BF16 = mybir.dt.bfloat16
ALU = mybir.AluOpType
ACT = mybir.ActivationFunctionType
AX_X = mybir.AxisListType.X

P = 128
B, S, E = 4, 1024, 128
H, HD = 16, 8
DC = 32
NE, INTER = 8, 256
EPS = 1e-5
SCALE = HD ** -0.5
NEG = -3.0e38

CT = 512
NT = CT // P
CHUNKS = B * S // CT
PAIRS = CHUNKS // 2
GH = 4
NG = H // GH
G = B * NG
QT = S // P
VW = HD + 1
ROWS = 9 * HD
MROWS = ROWS + 3
KROWS = 96
PAIR_OF_ONES = float(np.array([0x3F803F80], np.uint32).view(np.float32)[0])
DMA = 16


def exists(i, n):
    return not isinstance(i, int) or 0 <= i < n


def wait(eng, sem, value):
    if not isinstance(value, int) or value > 0:
        eng.wait_ge(sem, value)


def wait_apart(eng, sem, value, passed):
    wait(eng, sem, value)
    if not isinstance(value, int):
        eng.sem_inc(passed, 1)


def at_row(a, b):
    if isinstance(b, int):
        return a[b]
    dims = " ".join(f"d{i}" for i in range(1, len(a.shape)))
    return a[bass.ds(b, 1)].rearrange(f"d0 {dims} -> (d0 d1) {dims[3:]}")


def peeled(eng, n, body):
    body(0)
    with eng.Fori(1, n - 1) as i:
        body(i)
    body(n - 1)


STEPS = [
    (0, [(0, 0, 512, 0)]),
    (0, [(1, 128, 384, 0), (3, 384, 128, 384)]),
    (0, [(2, 256, 256, 0)]),
    (1, [(0, 512, 512, 0)]),
    (1, [(1, 512, 512, 0)]),
    (1, [(2, 512, 512, 0)]),
    (1, [(3, 512, 512, 0)]),
    (1, [(4, 512, 512, 0)]),
    (1, [(5, 640, 384, 0), (7, 896, 128, 384)]),
    (1, [(6, 768, 256, 0)]),
]
NS = len(STEPS)
HALF0 = 3
PTN = 4
LAG = 2
DIAGS = [[col for kt, q0, n, col in segs if q0 == kt * P] for _, segs in STEPS]
DIAG_UNTIL = [sum(len(d) for d in DIAGS[:s + 1]) for s in range(NS)]
NDIAG = DIAG_UNTIL[-1]
HEAD_ITEMS = [[(7, 0)], [(6, 0)], [(5, 0)], [(4, 0)], [(3, 0), (0, CT)], [(2, 0), (1, CT)]]
MAX_ITEMS = [(hh, tiles) for hh in range(GH) for tiles in HEAD_ITEMS]
NM = len(MAX_ITEMS)
EARLY = 8


def wide_items(g):
    if g == -1:
        seq = [("max", 1, i) for i in range(14)] + [("neg", 1, 0)] + [("max", 1, i) for i in range(14, NM)]
        seq += [("max", 2, i) for i in range(2)] + [("neg", 1, 1)] + [("max", 2, i) for i in range(2, EARLY)]
        return [seq]
    nxt = [("max", 1, i) for i in range(EARLY, NM)] if g + 1 < G else []
    neg = [("neg", 1, 0), ("neg", 1, 1)] if g + 1 < G else []
    early = [("max", 2, i) for i in range(EARLY)] if g + 2 < G else []
    prev = [("out", -1, 1)] if g > 0 else []
    seq = nxt[:11] + prev + neg[:1] + nxt[11:] + early[:1] + [("out", 0, 0)] + early[1:4] + neg[1:] + early[4:]
    slots, at = [[] for _ in range(GH * NS)], 0
    for i, item in enumerate(seq):
        at = max(at, i * (GH * NS - 1) // N_ITEMS)
        if item[0] == "out":
            at = max(at, GH * (LAG + 2 + (0 if item[2] else HALF0 - 1)))
        slots[at].append(item)
    return slots


N_FIRST = NM + 2 + EARLY
N_ITEMS = NM + 2 + 2


def items_before(g):
    if isinstance(g, int):
        return sum((len([i for s in wide_items(k) for i in s]) for k in range(-1, g)), 0)
    return N_FIRST - 1 + N_ITEMS * g


def like(g):
    return g if isinstance(g, int) else NG


def used_after(g, kind, off, which):
    flat = [i for slot in wide_items(like(g)) for i in slot]
    return items_before(g) + flat.index((kind, off, which)) + 1


def block_kernel(nc, x_d, wq_d, wqs_d, bq_d, wk_d, wks_d, bk_d, wkv_d, bkv_d, wv_d, bv_d, wo_d, bo_d,
                 zero_d, lns_d, lnb_d, gate_d, wg_d, wu_d, wd_d, swg_d, swu_d, swd_d, cos_d, sin_d, rev_d, out_d):
    qd = nc.dram_tensor("q_parts", (B, E, 3, S), BF16, kind="Internal").ap()
    kd = nc.dram_tensor("k_parts", (B, 3, E, 3, S), BF16, kind="Internal").ap()
    vd = nc.dram_tensor("v_ones", (B, P, QT, H * VW), F32, kind="Internal").ap()
    ad = nc.dram_tensor("attn", (B, NG, 2, P, NT, GH * HD), F32, kind="Internal").ap()
    wd = nc.dram_tensor("route", (2, NT * NE, P), F32, kind="Internal").ap()
    x_v = x_d.rearrange("b (h t p) e -> b h p t e", h=2, p=P)
    out_v = out_d.rearrange("b (h t p) e -> b h p t e", h=2, p=P)

    with ExitStack() as top:
        ps = top.enter_context(nc.psum_tensor("ps", [P, 8, CT], F32))
        psw = ps[:, :, :].rearrange("p b n -> p (b n)")

        def sb(stack, name, shape, dt=F32):
            return stack.enter_context(nc.sbuf_tensor(name, shape, dt))

        def sem(stack, name):
            return stack.enter_context(nc.semaphore(name))

        wg = sb(top, "wg", [P, NE + 1, INTER])
        wu = sb(top, "wu", [P, NE + 1, INTER])
        wdn = sb(top, "wdn", [P, NE + 1, 2, P])
        wo = sb(top, "wo", [P, E])
        bo_all = sb(top, "bo_all", [P, E])
        gate = sb(top, "gate", [P, NE])
        cols = sb(top, "cols", [P, 6])
        rev = sb(top, "rev", [P, NT * NE])
        identf = sb(top, "identf", [P, P])
        identb = sb(top, "identb", [P, P], BF16)
        neghalf = sb(top, "neghalf", [P, NT])
        RING = NG
        qr = sb(top, "qr", [KROWS, RING, GH, S], BF16)
        kr = sb(top, "kr", [KROWS, RING, GH, S], BF16)
        vr = sb(top, "vr", [P, RING, QT, GH * VW])
        mask = sb(top, "mask", [P, S])
        IN_DMAS = 8
        group_in = [sem(top, f"group_in{r}") for r in range(RING)]
        kr_ones = sem(top, "kr_ones")
        qr_zeros = sem(top, "qr_zeros")
        mask_ok = sem(top, "mask_ok")
        late_in = sem(top, "late_in")
        ident_ok = sem(top, "ident_ok")
        passed_dve, passed_pe, passed_pool, passed_sp = (sem(top, "passed_" + n) for n in ("dve", "pe", "pool", "sp"))
        LATE = 11

        def load_group(sp, b, r):
            cols = slice(r * GH * HD, (r + 1) * GH * HD)
            qg = at_row(qd, b)[cols].rearrange("(h d) s t -> (d s) h t", h=GH)
            for i in range(3):
                rows = slice(3 * HD * i, 3 * HD * (i + 1))
                kg = at_row(kd, b)[i, cols].rearrange("(h d) s t -> (d s) h t", h=GH)
                sp.dma_start(kr[rows, r], kg).then_inc(group_in[r], DMA)
                sp.dma_start(qr[rows, r], qg).then_inc(group_in[r], DMA)
            sp.dma_start(vr[:, r], at_row(vd, b)[:, :, r * GH * VW:(r + 1) * GH * VW]).then_inc(group_in[r], DMA)
            sp.dma_start(qr[ROWS:MROWS, r].rearrange("p h s -> p (h s)").bitcast(F32), zero_d).then_inc(group_in[r], DMA)

        def fill_kr(half):
            nc.vector.memset(kr[64:KROWS, 2 * half:2 * half + 2].rearrange("p r h s -> p (r h s)").bitcast(F32),
                             PAIR_OF_ONES).then_inc(kr_ones, 1)

        def fill_qr(half):
            nc.gpsimd.memset(qr[64:KROWS, 2 * half:2 * half + 2].rearrange("p r h s -> p (r h s)").bitcast(F32),
                             0.0).then_inc(qr_zeros, 1)

        def ln_stats(dve, steps, base, src, st, mv, ve):
            for t in range(NT):
                last = nc.vector.bn_stats(st[:, t, :], src[:, t, :])
            last.then_inc(steps, 1)
            wait_apart(dve, steps, base + 1, passed_dve)
            for t in range(NT):
                last = nc.vector.bn_aggr(mv[:, t, :], st[:, t, :])
            last.then_inc(steps, 1)
            dve.wait_ge(steps, base + 2)
            nc.vector.tensor_scalar_add(ve, mv[:, :, 1], EPS).then_inc(steps, 1)

        with ExitStack() as one:
            w_q = sb(one, "w_q", [P, E])
            w_qs = sb(one, "w_qs", [P, E])
            w_k = sb(one, "w_k", [P, E])
            w_ks = sb(one, "w_ks", [P, E])
            w_kv = sb(one, "w_kv", [P, DC])
            b_kv = sb(one, "b_kv", [DC, 1])
            w_v = sb(one, "w_v", [DC + 1, E])
            cos = sb(one, "cos", [P, S])
            sin = sb(one, "sin", [P, S])
            x1 = sb(one, "x_in", [P, 2, NT, E])
            st = sb(one, "st1", [P, 2, NT, 6])
            mv = sb(one, "mv1", [P, 2, NT, 2])
            ve = sb(one, "ve1", [P, 2, NT])
            rstd = sb(one, "rstd1", [P, 2, NT])
            xn = sb(one, "xn1", [P, 2, NT, E])
            xnT = sb(one, "xnT1", [P, 2, CT])
            ckvT = sb(one, "ckvT", [DC + 1, 2, CT])
            direct = sb(one, "direct", [P, 2, 2, CT])
            turned = sb(one, "turned", [P, 2, 2, CT])
            full = sb(one, "full", [P, 2, 2, CT])
            rest = sb(one, "rest", [P, 2, 2, CT])
            parts = sb(one, "parts", [P, 2, 2, 3, CT], BF16)
            v_st = sb(one, "v_st", [P, 2, NT, H * VW])

            w_in = sem(one, "w_in")
            x_ok = [sem(one, f"x_in{p}") for p in range(2)]
            ones_ok = sem(one, "ones_ok")
            one_row = sem(one, "one_row")
            ln = sem(one, "ln")
            xn_ok = sem(one, "xn_ok")
            rstd_ok = sem(one, "rstd_ok")
            xT_ready = sem(one, "xT_ready")
            xT_ok = sem(one, "xT_ok")
            proj = sem(one, "proj")
            ckv_ok = sem(one, "ckv_ok")
            rope = sem(one, "rope")
            added = sem(one, "added")
            gelu_ok = sem(one, "gelu_ok")
            rest_ok = sem(one, "rest_ok")
            mid_ok = sem(one, "mid_ok")
            low_ok = sem(one, "low_ok")
            v_ready = sem(one, "v_ready")
            v_ok = sem(one, "v_ok")
            stored = [sem(one, f"stored{p}") for p in range(2)]
            NSTORE = 7
            W_DMAS = 15
            B_XT, B_C, B_V = 0, 5, 6
            block = one.enter_context(nc.Block())

            @block.sync
            def _(sp):
                def load(j, p):
                    wait(sp, xn_ok, 2 * j + p - 1)
                    sp.dma_start(x1[:, p], at_row(x_v, j)[p]).then_inc(x_ok[p], DMA)

                load(0, 0)
                load(0, 1)

                def store(j, p):
                    c = 2 * j + p
                    at = slice(p * CT, (p + 1) * CT)
                    sp.wait_ge(v_ok, c + 1)
                    qb, kb, vb = at_row(qd, j), at_row(kd, j), at_row(vd, j)
                    sp.dma_start(vb[:, NT * p:NT * p + NT, :], v_st[:, p]).then_inc(stored[p], DMA)
                    sp.wait_ge(low_ok, 2 * c + 2)
                    sp.dma_start(qb[:, :, at], parts[:, p, 0]).then_inc(stored[p], DMA)
                    sp.dma_start(kb[0, :, :, at], parts[:, p, 1]).then_inc(stored[p], DMA)
                    for i in (1, 2):
                        sp.dma_start(kb[i, :, 0:3 - i, at], parts[:, p, 1, i:3]).then_inc(stored[p], DMA)
                        sp.dma_start(kb[i, :, 3 - i:3, at], parts[:, p, 1, 0:i]).then_inc(stored[p], DMA)

                def pair(j):
                    for p in range(2):
                        if exists(j + 1, PAIRS):
                            load(j + 1, p)
                        if exists(2 * j + p - 1, CHUNKS):
                            store(j - 1 + p, 1 - p)

                peeled(sp, PAIRS, pair)
                store(PAIRS - 1, 1)
                sp.wait_ge(kr_ones, 1)
                sp.wait_ge(qr_zeros, 1)
                sp.wait_ge(stored[0], DMA * NSTORE * PAIRS)
                load_group(sp, 0, 0)
                load_group(sp, 0, 1)
                sp.wait_ge(stored[1], DMA * NSTORE * PAIRS)

            @block.gpsimd
            def _(pool):
                nc.gpsimd.memset(neghalf[:], -0.5)
                nc.gpsimd.memset(identf[:], 0.0)
                nc.gpsimd.memset(identb[:], 0.0)
                nc.gpsimd.memset(v_st[:], 1.0).then_inc(ones_ok, 1)
                pool.wait_ge(ones_ok, 1)
                for m in (identf, identb):
                    last = nc.gpsimd.affine_select(out=m[:], in_=m[:], compare_op=ALU.not_equal, fill=1.0, base=0,
                                                   pattern=[[-1, P]], channel_multiplier=1)
                last.then_inc(ident_ok, 1)
                nc.gpsimd.memset(mask[:], 0.0).then_inc(mask_ok, 1)
                pool.wait_ge(mask_ok, 1)
                nc.gpsimd.affine_select(out=mask[:, S - P:], in_=mask[:, S - P:], compare_op=ALU.is_ge, fill=NEG, base=0,
                                        pattern=[[-1, P]], channel_multiplier=1).then_inc(mask_ok, 1)

                def root(c, p):
                    pool.wait_ge(ln, 3 * c + 3)
                    wait(pool, xn_ok, c - 1)
                    nc.gpsimd.tensor_tensor(rstd[:, p], ve[:, p], neghalf[:], ALU.pow).then_inc(rstd_ok, 1)

                def part_rest(c, p, i):
                    pool.wait_ge(gelu_ok, 4 * c + 2 * i + 2)
                    wait(pool, mid_ok, 2 * c - 2 + i)
                    nc.gpsimd.tensor_tensor(rest[:, p, i], full[:, p, i], parts[:, p, i, 0],
                                            ALU.subtract).then_inc(rest_ok, 1)

                def part_low(c, p, i):
                    pool.wait_ge(mid_ok, 2 * c + i + 1)
                    nc.gpsimd.tensor_tensor(parts[:, p, i, 2], rest[:, p, i], parts[:, p, i, 1],
                                            ALU.subtract).then_inc(low_ok, 1)

                root(0, 0)
                root(1, 1)
                pool.wait_ge(rstd_ok, 2)
                fill_qr(0)
                pool.wait_ge(qr_zeros, 1)

                def pair(j):
                    for p in range(2):
                        c = 2 * j + p
                        if exists(c - 1, CHUNKS):
                            part_rest(c - 1, 1 - p, 1)
                            part_low(c - 1, 1 - p, 0)
                            part_low(c - 1, 1 - p, 1)
                        if exists(c + 2, CHUNKS):
                            root(c + 2, p)
                        part_rest(c, p, 0)

                peeled(pool, PAIRS, pair)
                part_rest(CHUNKS - 1, 1, 1)
                for i in range(2):
                    part_low(CHUNKS - 1, 1, i)
                pool.wait_ge(low_ok, 2 * CHUNKS)
                fill_qr(1)
                pool.wait_ge(qr_zeros, 2)

            @block.scalar
            def _(act):
                for dst, src in ((cos[:], cos_d), (sin[:], sin_d), (w_kv[:], wkv_d), (w_q[:], wq_d), (w_qs[:], wqs_d),
                                 (w_k[:], wk_d), (w_ks[:], wks_d), (b_kv[:], bkv_d), (w_v[0:DC, :], wv_d),
                                 (w_v[DC:DC + 1, :], bv_d), (cols[:, 0:2], bq_d), (cols[:, 2:4], bk_d),
                                 (cols[:, 4:5], lns_d), (cols[:, 5:6], lnb_d), (rev[:], rev_d.partition_broadcast(P))):
                    act.dma_start(dst, src).then_inc(w_in, DMA)
                for dst, src in ((wg[:, 0:NE, :], wg_d.rearrange("e h i -> h e i")),
                                 (wu[:, 0:NE, :], wu_d.rearrange("e h i -> h e i")),
                                 (wg[:, NE, :], swg_d), (wu[:, NE, :], swu_d), (wo[:], wo_d),
                                 (bo_all[:], bo_d.partition_broadcast(P)), (gate[:], gate_d)):
                    act.dma_start(dst, src).then_inc(late_in, DMA)
                for i in range(2):
                    rows = slice(P * i, P * (i + 1))
                    act.dma_start(wdn[:, 0:NE, i, :], wd_d[:, rows, :].rearrange("e k h -> k e h")).then_inc(late_in, DMA)
                    act.dma_start(wdn[:, NE, i, :], swd_d[rows, :]).then_inc(late_in, DMA)

                def keep_xT(c, p):
                    act.wait_ge(xT_ready, c + 1)
                    wait(act, proj, 5 * (c - 1))
                    act.activation(xnT[:, p], ps[:, B_XT], ACT.Copy).then_inc(xT_ok, 1)

                keep_xT(0, 0)
                act.wait_ge(w_in, DMA * W_DMAS)
                act.wait_ge(ones_ok, 1)

                def part_mid(c, p, i):
                    act.wait_ge(rest_ok, 2 * c + i + 1)
                    act.activation(parts[:, p, i, 1], rest[:, p, i], ACT.Copy).then_inc(mid_ok, 1)

                def pair(j):
                    for p in range(2):
                        c = 2 * j + p
                        act.wait_ge(proj, 5 * c + 1)
                        wait(act, v_ready, c - 1)
                        act.activation(ckvT[0:DC, p], ps[0:DC, B_C], ACT.Gelu, bias=b_kv[:]).then_inc(ckv_ok, 1)
                        if exists(c - 1, CHUNKS):
                            part_mid(c - 1, 1 - p, 0)
                            part_mid(c - 1, 1 - p, 1)
                        if exists(c + 1, CHUNKS):
                            keep_xT(c + 1, 1 - p)
                        wait(act, stored[p], DMA * NSTORE * j)
                        for i in range(2):
                            act.wait_ge(added, 2 * c + i + 1)
                            if i == 0:
                                wait(act, rest_ok, 2 * c - 2)
                            act.activation(full[:, p, i], direct[:, p, i], ACT.Gelu).then_inc(gelu_ok, 1)
                            act.activation(parts[:, p, i, 0], direct[:, p, i], ACT.Gelu).then_inc(gelu_ok, 1)
                            if i == 0:
                                act.wait_ge(v_ready, c + 1)
                                act.activation(v_st[:, p].rearrange("p t (h w) -> p (t h) w", w=VW)[:, :, 0:HD],
                                               ps[:, B_V].rearrange("p (th w) -> p th w", w=HD), ACT.Copy).then_inc(v_ok, 1)

                peeled(act, PAIRS, pair)
                for i in range(2):
                    part_mid(CHUNKS - 1, 1, i)

            @block.vector
            def _(dve):
                def stats(j, p):
                    c = 2 * j + p
                    dve.wait_ge(x_ok[p], DMA * (j + 1))
                    ln_stats(dve, ln, 3 * c, x1[:, p], st[:, p], mv[:, p], ve[:, p])

                def normalize(c, p):
                    dve.wait_ge(rstd_ok, c + 1)
                    wait(dve, xT_ready, c - 1)
                    for t in range(NT):
                        last = nc.vector.tensor_scalar(xn[:, p, t], x1[:, p, t], mv[:, p, t, 0:1], rstd[:, p, t:t + 1],
                                                       ALU.subtract, ALU.mult)
                    last.then_inc(xn_ok, 1)

                nc.vector.memset(ckvT[DC:DC + 1, :, :], 1.0).then_inc(one_row, 1)
                stats(0, 0)
                normalize(0, 0)
                stats(0, 1)
                fill_kr(0)
                dve.wait_ge(w_in, DMA * W_DMAS)

                def pair(j):
                    for p in range(2):
                        c = 2 * j + p
                        if exists(c + 1, CHUNKS):
                            normalize(c + 1, 1 - p)
                        at = slice(p * CT, (p + 1) * CT)
                        wait(dve, gelu_ok, 4 * c - 4)
                        for i in range(4):
                            dst, table = ((direct, cos), (turned, sin))[i % 2]
                            dve.wait_ge(proj, 5 * c + 2 + i)
                            nc.vector.scalar_tensor_tensor(dst[:, p, i // 2], ps[:, 1 + i], cols[:, i:i + 1],
                                                           table[:, at], ALU.add, ALU.mult).then_inc(rope, 1)
                            if i % 2:
                                dve.wait_ge(rope, 4 * c + i + 1)
                                nc.vector.tensor_tensor(direct[:, p, i // 2], direct[:, p, i // 2],
                                                        turned[:, p, i // 2], ALU.add).then_inc(added, 1)
                        if exists(c + 2, CHUNKS):
                            stats(j + 1, p)

                peeled(dve, PAIRS, pair)
                fill_kr(1)

            @block.tensor
            def _(pe):
                def turn(c, p):
                    pe.wait_ge(xn_ok, c + 1)
                    wait(pe, xT_ok, c)
                    for t in range(NT):
                        last = nc.tensor.transpose(ps[:, B_XT, t * P:(t + 1) * P], xn[:, p, t], identf[:])
                    last.then_inc(xT_ready, 1)

                pe.wait_ge(ident_ok, 1)
                turn(0, 0)
                pe.wait_ge(w_in, DMA * W_DMAS)
                pe.wait_ge(one_row, 1)

                def pair(j):
                    for p in range(2):
                        c = 2 * j + p
                        pe.wait_ge(xT_ok, c + 1)
                        wait(pe, ckv_ok, c)
                        nc.tensor.matmul(ps[0:DC, B_C], w_kv[:], xnT[:, p], start=True, stop=True).then_inc(proj, 1)
                        for i, w in enumerate((w_q, w_qs, w_k, w_ks)):
                            wait(pe, rope, 4 * (c - 1) + 1 + i)
                            nc.tensor.matmul(ps[:, 1 + i], w[:], xnT[:, p], start=True, stop=True).then_inc(proj, 1)
                        if exists(c + 1, CHUNKS):
                            turn(c + 1, 1 - p)
                        pe.wait_ge(ckv_ok, c + 1)
                        wait(pe, v_ok, c)
                        for t in range(NT):
                            last = nc.tensor.matmul(ps[:, B_V, t * P:(t + 1) * P], ckvT[:, p, t * P:(t + 1) * P],
                                                    w_v[:], start=True, stop=True)
                        last.then_inc(v_ready, 1)

                peeled(pe, PAIRS, pair)
        with ExitStack() as two:
            expT = sb(two, "expT", [P, PTN, GH, CT])
            unread = sb(two, "unread", [P, 2, S], BF16)
            mx = sb(two, "mx", [P, 2, GH * QT])
            left = sb(two, "left", [P, 2, 2 * QT])
            negs = sb(two, "negs", [P, 2, 2, 2, 3, QT], BF16)
            negT = sb(two, "negT", [2 * 3 * QT, 2, P], BF16)
            oT = sb(two, "oT", [P, 2, CT])
            rsum = sb(two, "rsum", [P, 2, NT * GH])
            att = sb(two, "att", [P, 2, NT, GH * HD])

            zeroed = sem(two, "zeroed")
            neg_in = [[sem(two, f"neg_in{r}_{f}") for f in range(2)] for r in range(RING)]
            wide_ready = sem(two, "wide_ready")
            wide_used = sem(two, "wide_used")
            score_ready = sem(two, "score_ready")
            exp_ok = sem(two, "exp_ok")
            masked = sem(two, "masked")
            split = sem(two, "split")
            pv_done = sem(two, "pv_done")
            oT_ok = sem(two, "oT_ok")
            recip_ok = sem(two, "recip_ok")
            att_out = [sem(two, f"att_out{h}") for h in range(2)]
            B_S, B_O = 4, 6
            NEG_DMAS = 2
            block = two.enter_context(nc.Block())

            def batches(eng, body):
                def batch(b):
                    for r in range(NG):
                        g = NG * b + r
                        body(g, b, r, wide_items(like(g)))
                peeled(eng, B, batch)

            def shifted(b, r, d):
                return b + (r + d) // NG, (r + d) % NG

            def item_of(b, r, item):
                kind, off, which = item
                bb, rr = shifted(b, r, off)
                return kind, NG * bb + rr, bb, rr, which

            @block.sync
            def _(sp):
                def load(b, r):
                    wait(sp, pv_done, NS * (NG * b + r - RING + 1))
                    load_group(sp, b, r)

                sp.wait_ge(kr_ones, 2)
                sp.wait_ge(qr_zeros, 2)

                def store(b, r, half):
                    sp.dma_start(at_row(ad, b)[r, half], att[:, half]).then_inc(att_out[half], DMA)

                def place_neg(r, f):
                    for h in range(2):
                        sp.dma_start(qr[ROWS:MROWS, r, 2 * f + h, :],
                                     negT[3 * QT * h:3 * QT * (h + 1), f, :]).then_inc(neg_in[r][f], DMA)

                for f in range(2):
                    sp.wait_ge(wide_used, used_after(-1, "neg", 1, f))
                    place_neg(0, f)

                def body(g, b, r, slots):
                    if exists(g + 2, G):
                        load(*shifted(b, r, 2))
                    for item in [i for slot in slots for i in slot]:
                        kind, gg, bb, rr, which = item_of(b, r, item)
                        if kind != "max":
                            sp.wait_ge(wide_used, used_after(g, *item))
                        if kind == "out":
                            store(bb, rr, which)
                        elif kind == "neg":
                            place_neg(rr, which)

                batches(sp, body)
                sp.wait_ge(wide_used, items_before(G - 1) + 3)
                store(B - 1, NG - 1, 1)
                for half in range(2):
                    sp.wait_ge(att_out[half], DMA * G)

            @block.gpsimd
            def _(pool):
                def split_neg(g, par, f, seen):
                    wait_apart(pool, wide_used, seen, passed_pool)
                    base = 10 * g + 5 * f
                    m = mx[:, par, 2 * QT * f:2 * QT * (f + 1)]
                    n = [negs[:, par, f, :, s, :] for s in range(3)]
                    lf = left[:, f]
                    m3, l3 = (a.rearrange("p (h q) -> p h q", q=QT) for a in (m, lf))
                    nc.gpsimd.tensor_scalar(n[0], m3, -1.0, None, ALU.mult).then_inc(split, 1)
                    pool.wait_ge(split, base + 1)
                    nc.gpsimd.tensor_tensor(l3, m3, n[0], ALU.add).then_inc(split, 1)
                    wait_apart(pool, split, base + 2, passed_pool)
                    nc.gpsimd.tensor_scalar(n[1], l3, -1.0, None, ALU.mult).then_inc(split, 1)
                    pool.wait_ge(split, base + 3)
                    nc.gpsimd.tensor_tensor(l3, l3, n[1], ALU.add).then_inc(split, 1)
                    wait_apart(pool, split, base + 4, passed_pool)
                    nc.gpsimd.tensor_scalar(n[2], l3, -1.0, None, ALU.mult).then_inc(split, 1)

                for f in range(2):
                    split_neg(0, 0, f, used_after(-1, "max", 1, NM // 2 * (f + 1) - 1))

                def body(g, b, r, slots):
                    for s in range(NS):
                        if DIAGS[s]:
                            wait_apart(pool, exp_ok, GH * NS * g + GH * (s + 1), passed_pool)
                        for col in DIAGS[s]:
                            tile = expT[:, (NS * r + s) % PTN, :, col:col + P]
                            nc.gpsimd.affine_select(out=tile, in_=tile, compare_op=ALU.is_ge, fill=0.0, base=0,
                                                    pattern=[[0, GH], [1, P]], channel_multiplier=-1).then_inc(masked, 1)
                        if s in (HALF0, HALF0 + 3) and exists(g + 1, G):
                            f = int(s > HALF0)
                            split_neg(g + 1, (r + 1) % 2, f, used_after(g, "max", 1, NM // 2 * (f + 1) - 1))

                batches(pool, body)

            @block.scalar
            def _(act):
                def keep_out(g, half):
                    act.wait_ge(pv_done, NS * g + (HALF0, NS)[half])
                    if exists(g - 1, G):
                        act.wait_ge(wide_used, used_after(g, "out", -1, 1) if half else used_after(g - 1, "out", 0, 0))
                    act.activation(oT[:, half], ps[:, B_O + half], ACT.Copy).then_inc(oT_ok, 1)

                def body(g, b, r, slots):
                    for s in range(NS):
                        width = sum(n for _, _, n, _ in STEPS[s][1])
                        wait(act, pv_done, NS * g + s - PTN + 1)
                        for hh in range(GH):
                            n = GH * NS * g + GH * s + hh
                            act.wait_ge(score_ready, n + 1)
                            act.activation(expT[:, (NS * r + s) % PTN, hh, 0:width], ps[:, B_S + hh % 2, 0:width],
                                           ACT.Exp, scale=SCALE).then_inc(exp_ok, 1)
                        if s == LAG and exists(g - 1, G):
                            keep_out(g - 1, 1)
                        if s == HALF0 + LAG:
                            keep_out(g, 0)

                batches(act, body)
                keep_out(G - 1, 1)

            @block.vector
            def _(dve):
                nc.vector.memset(ps[:, B_O:B_O + 2, :], 0.0).then_inc(zeroed, 1)
                dve.wait_ge(mask_ok, 2)

                def item(n, odd, kind, g, bb, rr, which):
                    dve.wait_ge(wide_ready, n + 1)
                    if kind == "max":
                        hh, tiles = MAX_ITEMS[which]
                        if which == 0:
                            wait(dve, split, 10 * (g - 1))
                        wait_apart(dve, wide_used, n - 1, passed_dve)
                        for qi, col in tiles:
                            width = P * (qi + 1)
                            last = nc.vector.tensor_tensor_reduce(
                                out=unread[:, odd, col:col + width], in0=psw[:, 2 * CT * odd + col:2 * CT * odd + col + width],
                                in1=mask[:, S - width:], scale=1.0, scalar=NEG, op0=ALU.add, op1=ALU.max,
                                accum_out=mx[:, rr % 2, QT * hh + qi:QT * hh + qi + 1])
                        last.then_inc(wide_used, 1)
                    elif kind == "neg":
                        if exists(g - 1, G):
                            pb, pr = shifted(bb, rr, -1)
                            dve.wait_ge(neg_in[pr][which], NEG_DMAS * DMA * (pb + 1))
                        nc.vector.tensor_copy(negT[:, which, :], psw[0:6 * QT, 2 * CT * odd:2 * CT * odd + P // 2]
                                              .bitcast(BF16)).then_inc(wide_used, 1)
                    else:
                        o = ps[:, 2 * odd].rearrange("p (n w) -> p n w", w=32)
                        nc.vector.reciprocal(rsum[:, which], o[:, :, HD]).then_inc(recip_ok, 1)
                        dve.wait_ge(recip_ok, 2 * g + which + 1)
                        wait(dve, att_out[which], DMA * g)
                        nc.vector.tensor_tensor(att[:, which].rearrange("p t (h d) -> p (t h) d", d=HD), o[:, :, 0:HD],
                                                rsum[:, which].unsqueeze(2).to_broadcast([P, NT * GH, HD]),
                                                ALU.mult).then_inc(wide_used, 1)

                for k, i in enumerate(wide_items(-1)[0]):
                    item(k, k % 2, *item_of(-1, NG - 1, i))

                def body(g, b, r, slots):
                    for k, i in enumerate([i for slot in slots for i in slot]):
                        n = items_before(g) + k
                        item(n, (items_before(like(g)) + k) % 2, *item_of(b, r, i))

                batches(dve, body)
                n = items_before(G - 1) + 2
                item(n, n % 2, "out", G - 1, B - 1, NG - 1, 1)

            @block.tensor
            def _(pe):
                def item(n, odd, kind, g, bb, rr, which):
                    wait(pe, wide_used, n - 1)
                    if kind == "max":
                        hh, tiles = MAX_ITEMS[which]
                        if which == 0:
                            pe.wait_ge(group_in[rr], DMA * IN_DMAS * (bb + 1))
                        for qi, col in tiles:
                            width = P * (qi + 1)
                            for lo in range(0, width, CT):
                                hi = min(width, lo + CT)
                                at = 2 * CT * odd + col
                                last = nc.tensor.matmul(psw[:, at + lo:at + hi], qr[:, rr, hh, qi * P:(qi + 1) * P],
                                                        kr[:, rr, hh, lo:hi], start=True, stop=True)
                    elif kind == "neg":
                        wait_apart(pe, split, 10 * g + 5 * (which + 1), passed_pe)
                        last = nc.tensor.transpose(
                            psw[0:6 * QT, 2 * CT * odd:2 * CT * odd + P // 2].bitcast(BF16),
                            negs[:, rr % 2, which].rearrange("p h s q -> p (h s q)"), identb[:])
                    else:
                        pe.wait_ge(oT_ok, 2 * g + which + 1)
                        for t in range(NT):
                            last = nc.tensor.transpose(ps[:, 2 * odd, t * P:(t + 1) * P], oT[:, which, t * P:(t + 1) * P],
                                                       identf[:])
                    last.then_inc(wide_ready, 1)

                def product(g, r, s):
                    half, segs = STEPS[s]
                    first, end = s in (0, HALF0), s in (HALF0 - 1, NS - 1)
                    pe.wait_ge(exp_ok, GH * NS * g + GH * (s + 1))
                    if DIAGS[s]:
                        pe.wait_ge(masked, NDIAG * g + DIAG_UNTIL[s])
                    if first:
                        wait(pe, oT_ok, 2 * (g - 1) + half + 1)
                    for i, (kt, q0, n, col) in enumerate(segs):
                        at = q0 - CT * half
                        for hh in range(GH):
                            last = nc.tensor.matmul(
                                ps[32 * hh:32 * hh + VW, B_O + half, at:at + n], vr[:, r, kt, hh * VW:(hh + 1) * VW],
                                expT[:, (NS * r + s) % PTN, hh, col:col + n], start=first and i == 0,
                                stop=end and i == len(segs) - 1)
                    last.then_inc(pv_done, 1)

                for k, i in enumerate(wide_items(-1)[0]):
                    item(k, k % 2, *item_of(-1, NG - 1, i))
                pe.wait_ge(zeroed, 1)

                def body(g, b, r, slots):
                    k = 0
                    for s in range(NS):
                        for hh in range(GH):
                            n = GH * NS * g + GH * s + hh
                            if s == 0 and hh % 2 == 0:
                                pe.wait_ge(neg_in[r][hh // 2], NEG_DMAS * DMA * (b + 1))
                            wait(pe, exp_ok, n - 1)
                            for kt, q0, m, col in STEPS[s][1]:
                                last = nc.tensor.matmul(ps[:, B_S + hh % 2, col:col + m],
                                                        kr[:, r, hh, kt * P:(kt + 1) * P],
                                                        qr[:, r, hh, q0:q0 + m], start=True, stop=True)
                            last.then_inc(score_ready, 1)
                            for i in slots[GH * s + hh]:
                                item(items_before(g) + k, (items_before(like(g)) + k) % 2, *item_of(b, r, i))
                                k += 1
                        if s >= LAG:
                            product(g, r, s - LAG)
                        elif exists(g - 1, G):
                            product(g - 1, (r - 1) % NG, s - LAG + NS)

                batches(pe, body)
                for s in range(NS - LAG, NS):
                    product(G - 1, NG - 1, s)
                n = items_before(G - 1) + 2
                item(n, n % 2, "out", G - 1, B - 1, NG - 1, 1)
        with ExitStack() as three:
            at3 = sb(three, "at3", [P, 2, NT, E])
            x3 = sb(three, "x3", [P, 2, NT, E])
            atT = sb(three, "atT", [P, CT])
            proj_out = sb(three, "proj_out", [P, NT, E])
            x_mid = sb(three, "x_mid", [P, 2, NT, E])
            normed = sb(three, "normed", [P, NT, E])
            xf = sb(three, "xf", [P, NT, E])
            xr = sb(three, "xr", [P, NT, E])
            xfT = sb(three, "xfT", [P, 2, CT])
            xrT = sb(three, "xrT", [P, CT])
            st = sb(three, "st3", [P, 4, NT, 6])
            mv = sb(three, "mv3", [P, 4, NT, 2])
            ve = sb(three, "ve3", [P, 4, NT])
            rstd = sb(three, "rstd3", [P, 4, NT])
            lg = sb(three, "logits", [P, NT, NE])
            ex = sb(three, "exps", [P, NT, NE])
            pr = sb(three, "probs", [P, NT, NE])
            sc = sb(three, "scalars", [P, 9, NT])
            eq = sb(three, "equal", [P, 2, NT, NE])
            ri = sb(three, "ranked", [P, 2, NT, NE])
            oh = sb(three, "onehot", [P, 3, NT, NE])
            pm = sb(three, "unpicked", [P, NT, NE])
            pw = sb(three, "picked", [P, NT, NE])
            w_pad = sb(three, "w_pad", [P, P])
            wT = sb(three, "wT", [NT * NE, P])
            w_all = sb(three, "w_all", [P, 2, NE, CT])
            gs = sb(three, "gs", [P, 2, CT])
            hu = sb(three, "hu", [P, 4, CT])
            accT = sb(three, "accT", [P, CT])
            y = sb(three, "y", [P, NT, E])
            yo = sb(three, "yo", [P, 2, NT, E])

            chunk_in = [sem(three, f"chunk_in{p}") for p in range(2)]
            w_in3 = [sem(three, f"w_in3_{p}") for p in range(2)]
            w_out = sem(three, "w_out")
            y_out = [sem(three, f"y_out{p}") for p in range(2)]
            padded = sem(three, "padded")
            pre = sem(three, "pre")
            pre_rstd = sem(three, "pre_rstd")
            pre_pe = sem(three, "pre_pe")
            pre_act = sem(three, "pre_act")
            post = sem(three, "post")
            post_rstd = sem(three, "post_rstd")
            y_ready = sem(three, "y_ready")
            acc_ok = sem(three, "acc_ok")
            gate_ready = sem(three, "gate_ready")
            up_ready = sem(three, "up_ready")
            silu_ok = sem(three, "silu_ok")
            h_ok = sem(three, "h_ok")
            hw_ok = sem(three, "hw_ok")
            down = sem(three, "down")
            CHUNK_DMAS = NG + 1
            NX = NE + 1
            NH = 2 * NX
            (Y_PRE, LN_Y, X_MID, LN_X, LN_F, LG_MAX, LG_SUB, PICK) = (1, 5, 6, 10, 14, 15, 16, 36)
            K_PRE = PICK
            B_ACC, B_A, B_B, B_C = 4, 5, 6, 7
            block = three.enter_context(nc.Block())

            def steps3(eng, before, body, after):
                before()

                def pair(j):
                    for p in range(2):
                        body(2 * j + p, j, p)
                peeled(eng, PAIRS, pair)
                after()

            @block.sync
            def _(sp):
                def load(j, p):
                    c = 2 * j + p
                    wait(sp, pre, K_PRE * (c - 2) + X_MID)
                    wait(sp, pre_pe, 6 * (c - 2) + 1)
                    for hg in range(NG):
                        sp.dma_start(at3[:, p, :, hg * GH * HD:(hg + 1) * GH * HD],
                                     at_row(ad, j)[hg, p]).then_inc(chunk_in[p], DMA)
                    sp.dma_start(x3[:, p], at_row(x_v, j)[p]).then_inc(chunk_in[p], DMA)

                def spread_w(j, p):
                    c = 2 * j + p
                    sp.wait_ge(pre_act, 5 * c + 5)
                    sp.dma_start(wd[p], wT[:]).then_inc(w_out, DMA)
                    wait_apart(sp, w_out, DMA * (c + 1), passed_sp)
                    wait(sp, hw_ok, 2 * NE * (c - 1))
                    for e in range(NE):
                        sp.dma_start(w_all[:, p, e, :].rearrange("q (t n) -> q t n", n=P),
                                     wd[p].rearrange("(t e) n -> e t n", e=NE)[e].partition_broadcast(P)
                                     ).then_inc(w_in3[p], DMA)

                def store(j, p):
                    c = 2 * j + p
                    sp.wait_ge(post, 5 * c + 5)
                    sp.dma_start(at_row(out_v, j)[p], yo[:, p]).then_inc(y_out[p], DMA)

                def before():
                    load(0, 0)
                    load(0, 1)
                    spread_w(0, 0)

                def body(c, j, p):
                    if exists(c - 1, CHUNKS):
                        store(j - 1 + p, 1 - p)
                    if exists(c + 1, CHUNKS):
                        spread_w(j + p, 1 - p)
                    if exists(c + 2, CHUNKS):
                        load(j + 1, p)

                def after():
                    store(PAIRS - 1, 1)
                    for p in range(2):
                        sp.wait_ge(y_out[p], DMA * PAIRS)

                steps3(sp, before, body, after)

            @block.gpsimd
            def _(pool):
                def root(ready, count, k, done):
                    pool.wait_ge(ready, count)
                    nc.gpsimd.tensor_tensor(rstd[:, k], ve[:, k], neghalf[:], ALU.pow).then_inc(done, 1)

                def weigh(c, j, p, s):
                    for i in range(2):
                        n = NH * c + 2 * s + i
                        pool.wait_ge(h_ok, n + 1)
                        if i == 0:
                            pool.wait_ge(w_in3[p], DMA * (NE * j + NE))
                        nc.gpsimd.tensor_tensor(hu[:, (2 * s + i + 2 * p) % 4], hu[:, (2 * s + i + 2 * p) % 4],
                                                w_all[:, p, s - 1], ALU.mult).then_inc(hw_ok, 1)

                def before():
                    for k in range(3):
                        root(pre, (4, 9, 13)[k], k, pre_rstd)

                def body(c, j, p):
                    for s in range(NX):
                        if s > 0:
                            weigh(c, j, p, s)
                        if s == 1:
                            if exists(c - 1, CHUNKS):
                                root(post, 5 * (c - 1) + 3, 3, post_rstd)
                            if exists(c + 1, CHUNKS):
                                root(pre, K_PRE * (c + 1) + 4, 0, pre_rstd)
                        if s == 2 and exists(c + 1, CHUNKS):
                            root(pre, K_PRE * (c + 1) + 9, 1, pre_rstd)
                        if s == 3 and exists(c + 1, CHUNKS):
                            root(pre, K_PRE * (c + 1) + 13, 2, pre_rstd)

                def after():
                    root(post, 5 * (CHUNKS - 1) + 3, 3, post_rstd)

                steps3(pool, before, body, after)

            @block.scalar
            def _(act):
                def pre_a(c):
                    act.wait_ge(pre_pe, 6 * c + 1)
                    act.activation(atT[:], ps[:, B_A], ACT.Copy).then_inc(pre_act, 1)

                def pre_b(c, p):
                    act.wait_ge(pre_pe, 6 * c + 3)
                    act.activation(xfT[:, p], ps[:, B_A], ACT.Copy).then_inc(pre_act, 1)
                    act.wait_ge(pre_pe, 6 * c + 4)
                    act.activation(xrT[:], ps[:, B_B], ACT.Identity, scale=cols[:, 4:5],
                                   bias=cols[:, 5:6]).then_inc(pre_act, 1)

                def pre_c(c):
                    act.wait_ge(pre, K_PRE * c + LG_SUB)
                    act.activation(ex[:], lg[:], ACT.Exp).then_inc(pre_act, 1)

                def pre_d(c):
                    act.wait_ge(pre_pe, 6 * c + 6)
                    wait(act, w_out, DMA * c)
                    act.activation(wT[:], ps[0:NT * NE, B_A, 0:P], ACT.Copy).then_inc(pre_act, 1)

                def keep_acc(c):
                    act.wait_ge(down, NH * (c + 1))
                    act.activation(accT[:], ps[:, B_ACC], ACT.Copy).then_inc(acc_ok, 1)

                def before():
                    act.wait_ge(late_in, DMA * LATE)
                    pre_a(0)
                    pre_b(0, 0)
                    pre_c(0)
                    pre_d(0)

                def body(c, j, p):
                    for s in range(NX):
                        for i in range(2):
                            n = NH * c + 2 * s + i
                            act.wait_ge(gate_ready, n + 1)
                            wait(act, h_ok, n - 1)
                            act.activation(gs[:, i], ps[:, 2 * i], ACT.Silu).then_inc(silu_ok, 1)
                        if s == 0 and exists(c - 1, CHUNKS):
                            keep_acc(c - 1)
                        if exists(c + 1, CHUNKS):
                            if s == 0:
                                pre_a(c + 1)
                            if s == 4:
                                pre_b(c + 1, 1 - p)
                            if s == 5:
                                pre_c(c + 1)
                            if s == 7:
                                pre_d(c + 1)

                steps3(act, before, body, lambda: keep_acc(CHUNKS - 1))

            @block.vector
            def _(dve):
                v = nc.vector

                def normalize(out, src, k):
                    for t in range(NT):
                        last = v.tensor_scalar(out[:, t], src[:, t], mv[:, k, t, 0:1], rstd[:, k, t:t + 1],
                                               ALU.subtract, ALU.mult)
                    return last

                def pre_a(c):
                    dve.wait_ge(pre_pe, 6 * c + 2)
                    base = K_PRE * c
                    v.tensor_tensor(proj_out[:], ps[:, B_B].rearrange("p (t e) -> p t e", e=E),
                                    bo_all[:].unsqueeze(1).to_broadcast([P, NT, E]), ALU.add).then_inc(pre, 1)
                    dve.wait_ge(pre, base + Y_PRE)
                    ln_stats(dve, pre, base + Y_PRE, proj_out[:], st[:, 0], mv[:, 0], ve[:, 0])

                def pre_b(c, j, p):
                    base = K_PRE * c
                    dve.wait_ge(pre_rstd, 3 * c + 1)
                    normalize(normed, proj_out, 0).then_inc(pre, 1)
                    dve.wait_ge(pre, base + LN_Y)
                    dve.wait_ge(chunk_in[p], DMA * CHUNK_DMAS * (j + 1))
                    v.tensor_tensor(x_mid[:, p], x3[:, p], normed[:], ALU.add).then_inc(pre, 1)
                    dve.wait_ge(pre, base + X_MID)
                    ln_stats(dve, pre, base + X_MID, x_mid[:, p], st[:, 1], mv[:, 1], ve[:, 1])

                def pre_c(c, p):
                    base = K_PRE * c
                    dve.wait_ge(pre_rstd, 3 * c + 2)
                    normalize(xf, x_mid[:, p], 1).then_inc(pre, 1)
                    dve.wait_ge(pre, base + LN_X)
                    ln_stats(dve, pre, base + LN_X, xf[:], st[:, 2], mv[:, 2], ve[:, 2])
                    dve.wait_ge(pre_rstd, 3 * c + 3)
                    normalize(xr, xf, 2).then_inc(pre, 1)

                def over(k):
                    return sc[:, k].unsqueeze(2).to_broadcast([P, NT, NE])

                def pre_d(c):
                    base = K_PRE * c
                    dve.wait_ge(pre_pe, 6 * c + 5)
                    logits = ps[:, B_C, 0:NT * NE].rearrange("p (t e) -> p t e", e=NE)
                    v.reduce_max(sc[:, 0], logits, AX_X).then_inc(pre, 1)
                    dve.wait_ge(pre, base + LG_MAX)
                    v.tensor_tensor(lg[:], logits, over(0), ALU.subtract).then_inc(pre, 1)

                def pre_e(c):
                    dve.wait_ge(pre_act, 5 * c + 4)
                    rank = rev[:].rearrange("p (t e) -> p t e", e=NE)
                    at = K_PRE * c + LG_SUB
                    ops = [
                        lambda: v.reduce_sum(sc[:, 1], ex[:], AX_X),
                        lambda: v.reciprocal(sc[:, 2], sc[:, 1]),
                        lambda: v.tensor_tensor(pr[:], ex[:], over(2), ALU.mult),
                        lambda: v.reduce_max(sc[:, 3], pr[:], AX_X),
                        lambda: v.tensor_tensor(eq[:, 0], pr[:], over(3), ALU.is_equal),
                        lambda: v.tensor_tensor(ri[:, 0], eq[:, 0], rank, ALU.mult),
                        lambda: v.reduce_max(sc[:, 4], ri[:, 0], AX_X),
                        lambda: v.tensor_tensor(oh[:, 0], ri[:, 0], over(4), ALU.is_equal),
                        lambda: v.scalar_tensor_tensor(pm[:], oh[:, 0], -2.0, pr[:], ALU.mult, ALU.add),
                        lambda: v.reduce_max(sc[:, 5], pm[:], AX_X),
                        lambda: v.tensor_tensor(eq[:, 1], pm[:], over(5), ALU.is_equal),
                        lambda: v.tensor_tensor(ri[:, 1], eq[:, 1], rank, ALU.mult),
                        lambda: v.reduce_max(sc[:, 6], ri[:, 1], AX_X),
                        lambda: v.tensor_tensor(oh[:, 1], ri[:, 1], over(6), ALU.is_equal),
                        lambda: v.tensor_tensor(oh[:, 2], oh[:, 0], oh[:, 1], ALU.add),
                        lambda: v.tensor_tensor(pw[:], pr[:], oh[:, 2], ALU.mult),
                        lambda: v.tensor_tensor(sc[:, 7], sc[:, 3], sc[:, 5], ALU.add),
                        lambda: v.tensor_scalar_add(sc[:, 7], sc[:, 7], EPS),
                        lambda: v.reciprocal(sc[:, 8], sc[:, 7]),
                        lambda: v.tensor_tensor(w_pad[:, 0:NT * NE].rearrange("p (t e) -> p t e", e=NE), pw[:], over(8),
                                                ALU.mult),
                    ]
                    assert LG_SUB + len(ops) == K_PRE
                    for k, op in enumerate(ops):
                        if k:
                            dve.wait_ge(pre, at + k)
                        op().then_inc(pre, 1)

                def post_a(c):
                    dve.wait_ge(y_ready, c + 1)
                    ln_stats(dve, post, 5 * c, ps[:, B_C].rearrange("p (t e) -> p t e", e=E), st[:, 3], mv[:, 3], ve[:, 3])

                def post_b(c, j, p):
                    dve.wait_ge(post_rstd, c + 1)
                    normalize(y, ps[:, B_C].rearrange("p (t e) -> p t e", e=E), 3).then_inc(post, 1)
                    dve.wait_ge(post, 5 * c + 4)
                    wait(dve, y_out[p], DMA * j)
                    v.tensor_tensor(yo[:, p], y[:], x_mid[:, p], ALU.add).then_inc(post, 1)

                def before():
                    v.memset(w_pad[:], 0.0).then_inc(padded, 1)
                    dve.wait_ge(padded, 1)
                    dve.wait_ge(late_in, DMA * LATE)
                    pre_a(0)
                    pre_b(0, 0, 0)
                    pre_c(0, 0)
                    pre_d(0)
                    pre_e(0)

                def body(c, j, p):
                    for s in range(NX):
                        for i in range(2):
                            n = NH * c + 2 * s + i
                            dve.wait_ge(up_ready, n + 1)
                            dve.wait_ge(silu_ok, n + 1)
                            wait(dve, down, n - 3)
                            v.tensor_tensor(hu[:, (2 * s + i + 2 * p) % 4], gs[:, i], ps[:, 2 * i + 1],
                                            ALU.mult).then_inc(h_ok, 1)
                        if exists(c - 1, CHUNKS):
                            if s == 1:
                                post_a(c - 1)
                            if s == 2:
                                post_b(c - 1, j - 1 + p, 1 - p)
                        if exists(c + 1, CHUNKS):
                            if s == 1:
                                pre_a(c + 1)
                            if s == 2:
                                pre_b(c + 1, j + p, 1 - p)
                            if s == 3:
                                pre_c(c + 1, 1 - p)
                            if s == 5:
                                pre_d(c + 1)
                            if s == 6:
                                pre_e(c + 1)

                def after():
                    post_a(CHUNKS - 1)
                    post_b(CHUNKS - 1, PAIRS - 1, 1)

                steps3(dve, before, body, after)

            @block.tensor
            def _(pe):
                def turn(bank, src, ready, count, out, tiles=NT):
                    pe.wait_ge(ready, count)
                    for t in range(tiles):
                        last = nc.tensor.transpose(ps[:, bank, t * P:(t + 1) * P], src[:, t * P:(t + 1) * P], identf[:])
                    last.then_inc(out, 1)

                def flat(a):
                    return a.rearrange("p t e -> p (t e)")

                def pre_a(c, j, p):
                    wait(pe, pre_act, 5 * c)
                    turn(B_A, flat(at3[:, p]), chunk_in[p], DMA * CHUNK_DMAS * (j + 1), pre_pe)

                def pre_b(c):
                    pe.wait_ge(pre_act, 5 * c + 1)
                    for t in range(NT):
                        last = nc.tensor.matmul(ps[:, B_B, t * P:(t + 1) * P], atT[:, t * P:(t + 1) * P], wo[:],
                                                start=True, stop=True)
                    last.then_inc(pre_pe, 1)

                def pre_c(c):
                    turn(B_A, flat(xf[:]), pre, K_PRE * c + LN_X, pre_pe)
                    turn(B_B, flat(xr[:]), pre, K_PRE * c + LN_F, pre_pe)

                def pre_d(c):
                    pe.wait_ge(pre_act, 5 * c + 3)
                    for t in range(NT):
                        last = nc.tensor.matmul(ps[:, B_C, t * NE:(t + 1) * NE], xrT[:, t * P:(t + 1) * P], gate[:],
                                                start=True, stop=True)
                    last.then_inc(pre_pe, 1)

                def pre_e(c):
                    turn(B_A, w_pad, pre, K_PRE * (c + 1), pre_pe, 1)

                def down_product(c, p, s):
                    for i in range(2):
                        if s == 0:
                            if i == 0:
                                wait(pe, acc_ok, c)
                            pe.wait_ge(h_ok, NH * c + i + 1)
                        else:
                            pe.wait_ge(hw_ok, 2 * NE * c + 2 * (s - 1) + i + 1)
                        nc.tensor.matmul(ps[:, B_ACC], wdn[:, (s - 1) % NX, i], hu[:, (2 * s + i + 2 * p) % 4],
                                         start=s == 0 and i == 0, stop=s == NX - 1 and i == 1).then_inc(down, 1)

                def turn_y(c):
                    turn(B_C, accT, acc_ok, c + 1, y_ready)

                def before():
                    pe.wait_ge(late_in, DMA * LATE)
                    pre_a(0, 0, 0)
                    pre_b(0)
                    pre_c(0)
                    pre_d(0)
                    pre_e(0)

                def body(c, j, p):
                    for s in range(NX):
                        if s == 0:
                            pe.wait_ge(pre_act, 5 * c + 2)
                        for i in range(2):
                            n = NH * c + 2 * s + i
                            cols_i = slice(i * P, (i + 1) * P)
                            wait(pe, silu_ok, n - 1)
                            nc.tensor.matmul(ps[:, 2 * i], wg[:, (s - 1) % NX, cols_i], xfT[:, p],
                                             start=True, stop=True).then_inc(gate_ready, 1)
                            wait(pe, h_ok, n - 1)
                            nc.tensor.matmul(ps[:, 2 * i + 1], wu[:, (s - 1) % NX, cols_i], xfT[:, p],
                                             start=True, stop=True).then_inc(up_ready, 1)
                        if s > 0:
                            down_product(c, p, s - 1)
                        elif exists(c - 1, CHUNKS):
                            down_product(c - 1, 1 - p, NX - 1)
                        if s == 1 and exists(c - 1, CHUNKS):
                            turn_y(c - 1)
                        if exists(c + 1, CHUNKS):
                            if s == 0:
                                pre_a(c + 1, j + p, 1 - p)
                            if s == 1:
                                pre_b(c + 1)
                            if s == 4:
                                pre_c(c + 1)
                            if s == 5:
                                pre_d(c + 1)
                            if s == 7:
                                pre_e(c + 1)

                def after():
                    down_product(CHUNKS - 1, 1, NX - 1)
                    turn_y(CHUNKS - 1)

                steps3(pe, before, body, after)


def rotary_tables():
    inv = (np.float32(1.0) / np.float32(10000.0) ** (np.arange(0, E, 2, dtype=np.float32) / np.float32(E)))
    freqs = np.arange(S, dtype=np.float32)[:, None] * inv.astype(np.float32)[None, :]
    emb = np.concatenate([freqs, freqs], axis=-1)
    return np.cos(emb), np.sin(emb)


def kernel(**inputs):
    import concourse.bacc as bacc
    from concourse.bass_utils import run_bass_kernel_spmd

    a = {k: np.asarray(v) for k, v in inputs.items()}
    turned = (np.arange(E) + E // 2) % E
    cos, sin = rotary_tables()
    sign = np.where(np.arange(E) < E // 2, -1.0, 1.0).astype(np.float32)
    rev = np.tile(np.arange(NE, 0, -1, dtype=np.float32), NT)
    wq, bq, wk, bk = (a["L0_attn_" + n] for n in ("wqr", "bqr", "wkr", "bkr"))
    arrays = dict(
        x=a["L0_attn_x"], wq=wq, wqs=wq[:, turned], bq=np.stack([bq, bq[turned]], 1),
        wk=wk, wks=wk[:, turned], bk=np.stack([bk, bk[turned]], 1),
        wkv=a["L0_attn_wkv"], bkv=a["L0_attn_bkv"][:, None], wv=a["L0_attn_wv"], bv=a["L0_attn_bv"][None, :],
        wo=a["L0_attn_wo"], bo=a["L0_attn_bo"],
        zero=np.zeros((MROWS - ROWS, GH * S // 2), np.float32), lns=a["L0_ffn_ln_scale"][:, None], lnb=a["L0_ffn_ln_bias"][:, None],
        gate=a["L0_ffn_gate_w"].T, wg=a["L0_ffn_Wg"], wu=a["L0_ffn_Wu"], wd=a["L0_ffn_Wd"],
        swg=a["L0_ffn_sWg"], swu=a["L0_ffn_sWu"], swd=a["L0_ffn_sWd"],
        cos=cos.T, sin=(sin * sign).T, rev=rev,
    )
    nc = bacc.Bacc("TRN2", target_bir_lowering=False, num_devices=1)
    arrays = {f"in_{n}": np.ascontiguousarray(v) for n, v in arrays.items()}
    args = [nc.dram_tensor(n, v.shape, mybir.dt.from_np(v.dtype), kind="ExternalInput").ap() for n, v in arrays.items()]
    out = nc.dram_tensor("out", (B, S, E), F32, kind="ExternalOutput").ap()
    block_kernel(nc, *args, out)
    r = run_bass_kernel_spmd(nc, [arrays], core_ids=[0])
    return r.results[0]["out"]
```

```python
from contextlib import ExitStack

import numpy as np

import concourse.bass as bass
from concourse import mybir

F32 = mybir.dt.float32
F32R = mybir.dt.float32r
BF16 = mybir.dt.bfloat16
ALU = mybir.AluOpType
ACT = mybir.ActivationFunctionType
AX_X = mybir.AxisListType.X

P = 128
B, S, E = 4, 1024, 128
H, HD = 16, 8
DC = 32
NE, INTER = 8, 256
EPS = 1e-5
SCALE = HD ** -0.5
NEG = -3.0e38

CT = 512
NT = CT // P
CHUNKS = B * S // CT
PAIRS = CHUNKS // 2
GH = 4
NG = H // GH
G = B * NG
QT = S // P
VW = HD + 1
ROWS = 9 * HD
MROWS = ROWS + 3
KROWS = 96
PAIR_OF_ONES = float(np.array([0x3F803F80], np.uint32).view(np.float32)[0])
DMA = 16


def exists(i, n):
    return not isinstance(i, int) or 0 <= i < n


def wait(eng, sem, value):
    if not isinstance(value, int) or value > 0:
        eng.wait_ge(sem, value)


def wait_apart(eng, sem, value, passed):
    wait(eng, sem, value)
    if not isinstance(value, int):
        eng.sem_inc(passed, 1)


def at_row(a, b):
    if isinstance(b, int):
        return a[b]
    dims = " ".join(f"d{i}" for i in range(1, len(a.shape)))
    return a[bass.ds(b, 1)].rearrange(f"d0 {dims} -> (d0 d1) {dims[3:]}")


def peeled(eng, n, body):
    body(0)
    with eng.Fori(1, n - 1) as i:
        body(i)
    body(n - 1)


STEPS = [
    (0, [(0, 0, 512, 0)]),
    (0, [(1, 128, 384, 0), (3, 384, 128, 384)]),
    (0, [(2, 256, 256, 0)]),
    (1, [(0, 512, 512, 0)]),
    (1, [(1, 512, 512, 0)]),
    (1, [(2, 512, 512, 0)]),
    (1, [(3, 512, 512, 0)]),
    (1, [(4, 512, 512, 0)]),
    (1, [(5, 640, 384, 0), (7, 896, 128, 384)]),
    (1, [(6, 768, 256, 0)]),
]
NS = len(STEPS)
HALF0 = 3
PTN = 4
LAG = 2
DIAGS = [[col for kt, q0, n, col in segs if q0 == kt * P] for _, segs in STEPS]
DIAG_UNTIL = [sum(len(d) for d in DIAGS[:s + 1]) for s in range(NS)]
NDIAG = DIAG_UNTIL[-1]
HEAD_ITEMS = [[(7, 0)], [(6, 0)], [(5, 0)], [(4, 0)], [(3, 0), (0, CT)], [(2, 0), (1, CT)]]
MAX_ITEMS = [(hh, tiles) for hh in range(GH) for tiles in HEAD_ITEMS]
NM = len(MAX_ITEMS)
EARLY = 8
IN_ONE = 18


def wide_items(g):
    if g == -1:
        seq = [("max", 1, i) for i in range(NM)]
        return [seq[:IN_ONE + 1] + [("neg", 1, 0)] + seq[IN_ONE + 1:] + [("neg", 1, 1)]]
    nxt = [("max", 1, i) for i in range(0 if g == 0 else EARLY, NM)] if g + 1 < G else []
    neg = [("neg", 1, 0), ("neg", 1, 1)] if g + 1 < G else []
    early = [("max", 2, i) for i in range(EARLY)] if g + 2 < G else []
    prev = [("out", -1, 1)] if g > 0 else []
    if g == 0:
        seq = nxt[:17] + neg[:1] + nxt[17:22] + [("out", 0, 0)] + nxt[22:] + early[:4] + neg[1:] + early[4:]
    else:
        seq = nxt[:11] + prev + neg[:1] + nxt[11:] + early[:1] + [("out", 0, 0)] + early[1:4] + neg[1:] + early[4:]
    slots, at = [[] for _ in range(GH * NS)], 0
    for i, item in enumerate(seq):
        at = max(at, i * (GH * NS - 1) // max(N_ITEMS, len(seq)))
        if item[0] == "out":
            at = max(at, GH * (LAG + 2 + (0 if item[2] else HALF0 - 1)))
        slots[at].append(item)
    return slots


N_FIRST = NM + 2
N_ITEMS = NM + 2 + 2


def items_before(g):
    if isinstance(g, int):
        return sum((len([i for s in wide_items(k) for i in s]) for k in range(-1, g)), 0)
    return N_FIRST + EARLY - 1 + N_ITEMS * g


def like(g):
    return g if isinstance(g, int) else NG


def used_after(g, kind, off, which):
    flat = [i for slot in wide_items(like(g)) for i in slot]
    return items_before(g) + flat.index((kind, off, which)) + 1


def block_kernel(nc, x_d, wq_d, wqs_d, bq_d, wk_d, wks_d, bk_d, wkv_d, bkv_d, wv_d, bv_d, wo_d, bo_d,
                 zero_d, lns_d, lnb_d, gate_d, wg_d, wu_d, wd_d, swg_d, swu_d, swd_d, cos_d, sin_d, rev_d, out_d):
    qd = nc.dram_tensor("q_parts", (B, E, 3, S), BF16, kind="Internal").ap()
    kd = nc.dram_tensor("k_parts", (B, 3, E, 3, S), BF16, kind="Internal").ap()
    vd = nc.dram_tensor("v_ones", (B, P, QT, H * VW), F32, kind="Internal").ap()
    ad = nc.dram_tensor("attn", (B, NG, 2, P, NT, GH * HD), F32, kind="Internal").ap()
    wd = nc.dram_tensor("route", (2, NT * NE, P), F32, kind="Internal").ap()
    x_v = x_d.rearrange("b (h t p) e -> b h p t e", h=2, p=P)
    out_v = out_d.rearrange("b (h t p) e -> b h p t e", h=2, p=P)

    with ExitStack() as top:
        ps = top.enter_context(nc.psum_tensor("ps", [P, 8, CT], F32))
        psw = ps[:, :, :].rearrange("p b n -> p (b n)")

        def sb(stack, name, shape, dt=F32):
            return stack.enter_context(nc.sbuf_tensor(name, shape, dt))

        def sem(stack, name):
            return stack.enter_context(nc.semaphore(name))

        w_gu = sb(top, "w_gu", [P, 2, NE + 1, INTER])
        wdn = sb(top, "wdn", [P, NE + 1, 2, P])
        w_hi = sb(top, "w_hi", [P, 2, NE + 1, INTER], F32R)
        w_lo = sb(top, "w_lo", [P, 2, NE + 1, INTER], F32R)
        wo = sb(top, "wo", [P, E])
        bo_all = sb(top, "bo_all", [P, E])
        gate = sb(top, "gate", [P, NE])
        cols = sb(top, "cols", [P, 6])
        rev = sb(top, "rev", [P, NT * NE])
        identf = sb(top, "identf", [P, P])
        identb = sb(top, "identb", [P, P], BF16)
        neghalf = sb(top, "neghalf", [P, NT])
        RING = NG
        mid = ExitStack()
        qr = sb(mid, "qr", [KROWS, RING, GH, S], BF16)
        kr = sb(mid, "kr", [KROWS, RING, GH, S], BF16)
        vr = sb(mid, "vr", [P, RING, QT, GH * VW])
        mask = sb(mid, "mask", [P, S])
        x1 = sb(mid, "x_in", [P, 2, NT, E])
        unread = x1[:].rearrange("p h t e -> p h (t e)").bitcast(BF16)
        mx = sb(mid, "mx", [P, 2, GH * QT])
        wide_ready = sem(top, "wide_ready")
        wide_used = sem(top, "wide_used")
        IN_DMAS = 8
        group_in = [sem(top, f"group_in{r}") for r in range(RING)]
        kr_ones = sem(top, "kr_ones")
        qr_zeros = sem(top, "qr_zeros")
        mask_ok = sem(top, "mask_ok")
        late_in = sem(top, "late_in")
        ident_ok = sem(top, "ident_ok")
        passed_dve, passed_pe, passed_pool, passed_sp = (sem(top, "passed_" + n) for n in ("dve", "pe", "pool", "sp"))
        LATE = 14

        def load_group(sp, b, r):
            cols = slice(r * GH * HD, (r + 1) * GH * HD)
            qg = at_row(qd, b)[cols].rearrange("(h d) s t -> (d s) h t", h=GH)
            for i in range(3):
                rows = slice(3 * HD * i, 3 * HD * (i + 1))
                kg = at_row(kd, b)[i, cols].rearrange("(h d) s t -> (d s) h t", h=GH)
                sp.dma_start(kr[rows, r], kg).then_inc(group_in[r], DMA)
                sp.dma_start(qr[rows, r], qg).then_inc(group_in[r], DMA)
            sp.dma_start(vr[:, r], at_row(vd, b)[:, :, r * GH * VW:(r + 1) * GH * VW]).then_inc(group_in[r], DMA)
            sp.dma_start(qr[ROWS:MROWS, r].rearrange("p h s -> p (h s)").bitcast(F32), zero_d).then_inc(group_in[r], DMA)

        def scores_for_max(pe, odd, rr, which):
            hh, tiles = MAX_ITEMS[which]
            for qi, col in tiles:
                width = P * (qi + 1)
                for lo in range(0, width, CT):
                    hi = min(width, lo + CT)
                    at = 2 * CT * odd + col
                    last = nc.tensor.matmul(psw[:, at + lo:at + hi], qr[:, rr, hh, qi * P:(qi + 1) * P],
                                            kr[:, rr, hh, lo:hi], start=True, stop=True)
            last.then_inc(wide_ready, 1)

        def maxima(dve, n, odd, rr, which):
            hh, tiles = MAX_ITEMS[which]
            wait_apart(dve, wide_used, n - 1, passed_dve)
            for qi, col in tiles:
                width = P * (qi + 1)
                last = nc.vector.tensor_tensor_reduce(
                    out=unread[:, odd, col:col + width], in0=psw[:, 2 * CT * odd + col:2 * CT * odd + col + width],
                    in1=mask[:, S - width:], scale=1.0, scalar=NEG, op0=ALU.add, op1=ALU.max,
                    accum_out=mx[:, rr % 2, QT * hh + qi:QT * hh + qi + 1])
            last.then_inc(wide_used, 1)

        def ln_stats(dve, steps, base, src, st, mv, ve):
            for t in range(NT):
                last = nc.vector.bn_stats(st[:, t, :], src[:, t, :])
            last.then_inc(steps, 1)
            wait_apart(dve, steps, base + 1, passed_dve)
            for t in range(NT):
                last = nc.vector.bn_aggr(mv[:, t, :], st[:, t, :])
            last.then_inc(steps, 1)
            dve.wait_ge(steps, base + 2)
            nc.vector.tensor_scalar_add(ve, mv[:, :, 1], EPS).then_inc(steps, 1)

        with ExitStack() as one:
            w_q = sb(one, "w_q", [P, E])
            w_qs = sb(one, "w_qs", [P, E])
            w_k = sb(one, "w_k", [P, E])
            w_ks = sb(one, "w_ks", [P, E])
            w_kv = sb(one, "w_kv", [P, DC])
            b_kv = sb(one, "b_kv", [DC, 1])
            w_v = sb(one, "w_v", [DC + 1, E])
            cos = sb(one, "cos", [P, S])
            sin = sb(one, "sin", [P, S])
            st = sb(one, "st1", [P, 2, NT, 6])
            mv = sb(one, "mv1", [P, 2, NT, 2])
            ve = sb(one, "ve1", [P, 2, NT])
            rstd = sb(one, "rstd1", [P, 2, NT])
            xnT = sb(one, "xnT1", [P, 2, CT])
            ckvT = sb(one, "ckvT", [DC + 1, 2, CT])
            direct = sb(one, "direct", [P, 2, 2, CT])
            turned = sb(one, "turned", [P, 2, CT])
            full = sb(one, "full", [P, 2, 2, CT])
            rest = sb(one, "rest", [P, 2, 2, CT])
            parts = sb(one, "parts", [P, 2, 2, 3, CT], BF16)
            v_st = sb(one, "v_st", [P, 2, NT, H * VW])

            w_in = sem(one, "w_in")
            tables_in = sem(one, "tables_in")
            x_ok = [sem(one, f"x_in{p}") for p in range(2)]
            ones_ok = sem(one, "ones_ok")
            one_row = sem(one, "one_row")
            ln = sem(one, "ln")
            xn_ok = sem(one, "xn_ok")
            rstd_ok = sem(one, "rstd_ok")
            xT_ready = sem(one, "xT_ready")
            xT_ok = sem(one, "xT_ok")
            proj = sem(one, "proj")
            ckv_ok = sem(one, "ckv_ok")
            rope = sem(one, "rope")
            added = sem(one, "added")
            gelu_ok = sem(one, "gelu_ok")
            rest_ok = sem(one, "rest_ok")
            mid_ok = sem(one, "mid_ok")
            low_ok = sem(one, "low_ok")
            v_ready = sem(one, "v_ready")
            v_ok = sem(one, "v_ok")
            stored = [sem(one, f"stored{p}") for p in range(2)]
            NSTORE = 7
            W_DMAS = 10
            B_XT, B_C, B_V = 0, 5, 6
            block = one.enter_context(nc.Block())

            @block.sync
            def _(sp):
                def load(j, p):
                    wait(sp, xT_ready, 2 * j + p - 1)
                    sp.dma_start(x1[:, p], at_row(x_v, j)[p]).then_inc(x_ok[p], DMA)

                load(0, 0)
                for dst, src in ((cos[:], cos_d), (sin[:], sin_d)):
                    sp.dma_start(dst, src).then_inc(tables_in, DMA)
                load(0, 1)
                sp.wait_ge(w_in, DMA * W_DMAS)
                for dst, src in ((wo[:], wo_d), (bo_all[:], bo_d.partition_broadcast(P)), (gate[:], gate_d),
                                 (cols[:, 4:5], lns_d), (cols[:, 5:6], lnb_d), (rev[:], rev_d.partition_broadcast(P)),
                                 (w_gu[:, 0, 0:NE, :], wg_d.rearrange("e h i -> h e i")),
                                 (w_gu[:, 1, 0:NE, :], wu_d.rearrange("e h i -> h e i")),
                                 (w_gu[:, 0, NE, :], swg_d), (w_gu[:, 1, NE, :], swu_d)):
                    sp.dma_start(dst, src).then_inc(late_in, DMA)
                for i in range(2):
                    rows = slice(P * i, P * (i + 1))
                    sp.dma_start(wdn[:, 0:NE, i, :], wd_d[:, rows, :].rearrange("e k h -> k e h")).then_inc(late_in, DMA)
                    sp.dma_start(wdn[:, NE, i, :], swd_d[rows, :]).then_inc(late_in, DMA)

                def store(j, p):
                    c = 2 * j + p
                    at = slice(p * CT, (p + 1) * CT)
                    sp.wait_ge(v_ok, c + 1)
                    qb, kb, vb = at_row(qd, j), at_row(kd, j), at_row(vd, j)
                    sp.dma_start(vb[:, NT * p:NT * p + NT, :], v_st[:, p]).then_inc(stored[p], DMA)
                    sp.wait_ge(low_ok, 2 * c + 2)
                    sp.dma_start(qb[:, :, at], parts[:, p, 0]).then_inc(stored[p], DMA)
                    sp.dma_start(kb[0, :, :, at], parts[:, p, 1]).then_inc(stored[p], DMA)
                    for i in (1, 2):
                        sp.dma_start(kb[i, :, 0:3 - i, at], parts[:, p, 1, i:3]).then_inc(stored[p], DMA)
                        sp.dma_start(kb[i, :, 3 - i:3, at], parts[:, p, 1, 0:i]).then_inc(stored[p], DMA)

                def pair(j):
                    for p in range(2):
                        if exists(j + 1, PAIRS):
                            load(j + 1, p)
                        else:
                            if p == 0:
                                sp.wait_ge(kr_ones, 1)
                                sp.wait_ge(qr_zeros, 1)
                                for i in range(2):
                                    sp.wait_ge(stored[i], DMA * NSTORE)
                            load_group(sp, 0, p)
                        if exists(2 * j + p - 1, CHUNKS):
                            store(j - 1 + p, 1 - p)

                peeled(sp, PAIRS, pair)
                store(PAIRS - 1, 1)
                for p in range(2):
                    sp.wait_ge(stored[p], DMA * NSTORE * PAIRS)

            @block.gpsimd
            def _(pool):
                nc.gpsimd.memset(neghalf[:], -0.5)
                nc.gpsimd.memset(identf[:], 0.0)
                nc.gpsimd.memset(identb[:], 0.0)
                nc.gpsimd.memset(v_st[:], 1.0).then_inc(ones_ok, 1)
                pool.wait_ge(ones_ok, 1)
                for m in (identf, identb):
                    last = nc.gpsimd.affine_select(out=m[:], in_=m[:], compare_op=ALU.not_equal, fill=1.0, base=0,
                                                   pattern=[[-1, P]], channel_multiplier=1)
                last.then_inc(ident_ok, 1)
                nc.gpsimd.memset(mask[:], 0.0).then_inc(mask_ok, 1)
                pool.wait_ge(mask_ok, 1)
                nc.gpsimd.affine_select(out=mask[:, S - P:], in_=mask[:, S - P:], compare_op=ALU.is_ge, fill=NEG, base=0,
                                        pattern=[[-1, P]], channel_multiplier=1).then_inc(mask_ok, 1)

                def root(c, p):
                    pool.wait_ge(ln, 3 * c + 3)
                    wait(pool, xn_ok, c - 1)
                    nc.gpsimd.tensor_tensor(rstd[:, p], ve[:, p], neghalf[:], ALU.pow).then_inc(rstd_ok, 1)

                def part_rest(c, p, i):
                    pool.wait_ge(gelu_ok, 4 * c + 2 * i + 2)
                    wait(pool, mid_ok, 2 * c - 2 + i)
                    nc.gpsimd.tensor_tensor(rest[:, p, i], full[:, p, i], parts[:, p, i, 0],
                                            ALU.subtract).then_inc(rest_ok, 1)

                def part_low(c, p, i):
                    pool.wait_ge(mid_ok, 2 * c + i + 1)
                    nc.gpsimd.tensor_tensor(parts[:, p, i, 2], rest[:, p, i], parts[:, p, i, 1],
                                            ALU.subtract).then_inc(low_ok, 1)

                root(0, 0)
                root(1, 1)
                pool.wait_ge(rstd_ok, 2)
                nc.gpsimd.memset(qr[64:KROWS].rearrange("p r h s -> p (r h s)").bitcast(F32),
                                 0.0).then_inc(qr_zeros, 1)
                pool.wait_ge(qr_zeros, 1)

                def pair(j):
                    for p in range(2):
                        c = 2 * j + p
                        if exists(c - 1, CHUNKS):
                            part_rest(c - 1, 1 - p, 1)
                            part_low(c - 1, 1 - p, 0)
                            part_low(c - 1, 1 - p, 1)
                        if exists(c + 2, CHUNKS):
                            root(c + 2, p)
                        part_rest(c, p, 0)

                peeled(pool, PAIRS, pair)
                part_rest(CHUNKS - 1, 1, 1)
                for i in range(2):
                    part_low(CHUNKS - 1, 1, i)

            @block.scalar
            def _(act):
                for dst, src in ((w_kv[:], wkv_d), (w_q[:], wq_d), (b_kv[:], bkv_d), (cols[:, 0:2], bq_d),
                                 (w_qs[:], wqs_d), (w_k[:], wk_d), (w_ks[:], wks_d), (cols[:, 2:4], bk_d),
                                 (w_v[0:DC, :], wv_d), (w_v[DC:DC + 1, :], bv_d)):
                    act.dma_start(dst, src).then_inc(w_in, DMA)

                def keep_xT(c, p):
                    act.wait_ge(xT_ready, c + 1)
                    wait(act, proj, 5 * (c - 1))
                    act.activation(xnT[:, p], ps[:, B_XT], ACT.Copy).then_inc(xT_ok, 1)

                keep_xT(0, 0)
                act.wait_ge(w_in, DMA * W_DMAS)
                act.wait_ge(ones_ok, 1)

                def part_mid(c, p, i):
                    act.wait_ge(rest_ok, 2 * c + i + 1)
                    act.activation(parts[:, p, i, 1], rest[:, p, i], ACT.Copy).then_inc(mid_ok, 1)

                def pair(j):
                    for p in range(2):
                        c = 2 * j + p
                        act.wait_ge(proj, 5 * c + 1)
                        wait(act, v_ready, c - 1)
                        act.activation(ckvT[0:DC, p], ps[0:DC, B_C], ACT.Gelu, bias=b_kv[:]).then_inc(ckv_ok, 1)
                        if exists(c - 1, CHUNKS):
                            part_mid(c - 1, 1 - p, 0)
                            part_mid(c - 1, 1 - p, 1)
                        if exists(c + 1, CHUNKS):
                            keep_xT(c + 1, 1 - p)
                        wait(act, stored[p], DMA * NSTORE * j)
                        for i in range(2):
                            act.wait_ge(added, 2 * c + i + 1)
                            if i == 0:
                                wait(act, rest_ok, 2 * c - 2)
                            act.activation(full[:, p, i], direct[:, p, i], ACT.Gelu).then_inc(gelu_ok, 1)
                            act.activation(parts[:, p, i, 0], direct[:, p, i], ACT.Gelu).then_inc(gelu_ok, 1)
                            if i == 0:
                                act.wait_ge(v_ready, c + 1)
                                act.activation(v_st[:, p].rearrange("p t (h w) -> p (t h) w", w=VW)[:, :, 0:HD],
                                               ps[:, B_V].rearrange("p (th w) -> p th w", w=HD), ACT.Copy).then_inc(v_ok, 1)

                peeled(act, PAIRS, pair)
                for i in range(2):
                    part_mid(CHUNKS - 1, 1, i)

            @block.vector
            def _(dve):
                def stats(j, p):
                    c = 2 * j + p
                    dve.wait_ge(x_ok[p], DMA * (j + 1))
                    ln_stats(dve, ln, 3 * c, x1[:, p], st[:, p], mv[:, p], ve[:, p])

                def normalize(c, p):
                    dve.wait_ge(rstd_ok, c + 1)
                    for t in range(NT):
                        last = nc.vector.tensor_scalar(x1[:, p, t], x1[:, p, t], mv[:, p, t, 0:1], rstd[:, p, t:t + 1],
                                                       ALU.subtract, ALU.mult)
                    last.then_inc(xn_ok, 1)

                nc.vector.memset(ckvT[DC:DC + 1, :, :], 1.0).then_inc(one_row, 1)
                stats(0, 0)
                normalize(0, 0)
                stats(0, 1)
                nc.vector.memset(kr[64:KROWS].rearrange("p r h s -> p (r h s)").bitcast(F32),
                                 PAIR_OF_ONES).then_inc(kr_ones, 1)
                dve.wait_ge(w_in, DMA * W_DMAS)
                dve.wait_ge(tables_in, DMA * 2)

                def pair(j):
                    for p in range(2):
                        c = 2 * j + p
                        if exists(c + 1, CHUNKS):
                            normalize(c + 1, 1 - p)
                        at = slice(p * CT, (p + 1) * CT)
                        wait(dve, gelu_ok, 4 * c - 4)
                        for i in range(4):
                            dst, table = ((direct[:, p, i // 2], cos), (turned[:, i // 2], sin))[i % 2]
                            if i % 2:
                                wait(dve, added, 2 * c + i // 2 - 1)
                            dve.wait_ge(proj, 5 * c + 2 + i)
                            nc.vector.scalar_tensor_tensor(dst, ps[:, 1 + i], cols[:, i:i + 1],
                                                           table[:, at], ALU.add, ALU.mult).then_inc(rope, 1)
                            if i % 2:
                                dve.wait_ge(rope, 4 * c + i + 1)
                                nc.vector.tensor_tensor(direct[:, p, i // 2], direct[:, p, i // 2],
                                                        turned[:, i // 2], ALU.add).then_inc(added, 1)
                        if exists(c + 2, CHUNKS):
                            stats(j + 1, p)

                peeled(dve, PAIRS, pair)
                dve.wait_ge(mask_ok, 2)
                dve.wait_ge(xT_ready, CHUNKS)
                for k in range(IN_ONE):
                    dve.wait_ge(wide_ready, k + 1)
                    maxima(dve, k, k % 2, 0, k)

            @block.tensor
            def _(pe):
                def turn(c, p):
                    pe.wait_ge(xn_ok, c + 1)
                    wait(pe, xT_ok, c)
                    for t in range(NT):
                        last = nc.tensor.transpose(ps[:, B_XT, t * P:(t + 1) * P], x1[:, p, t], identf[:])
                    last.then_inc(xT_ready, 1)

                pe.wait_ge(ident_ok, 1)
                turn(0, 0)
                pe.wait_ge(w_in, DMA * W_DMAS)
                pe.wait_ge(one_row, 1)

                def pair(j):
                    for p in range(2):
                        c = 2 * j + p
                        pe.wait_ge(xT_ok, c + 1)
                        wait(pe, ckv_ok, c)
                        nc.tensor.matmul(ps[0:DC, B_C], w_kv[:], xnT[:, p], start=True, stop=True).then_inc(proj, 1)
                        for i, w in enumerate((w_q, w_qs, w_k, w_ks)):
                            wait(pe, rope, 4 * (c - 1) + 1 + i)
                            nc.tensor.matmul(ps[:, 1 + i], w[:], xnT[:, p], start=True, stop=True).then_inc(proj, 1)
                        if exists(c + 1, CHUNKS):
                            turn(c + 1, 1 - p)
                        pe.wait_ge(ckv_ok, c + 1)
                        wait(pe, v_ok, c)
                        for t in range(NT):
                            last = nc.tensor.matmul(ps[:, B_V, t * P:(t + 1) * P], ckvT[:, p, t * P:(t + 1) * P],
                                                    w_v[:], start=True, stop=True)
                        last.then_inc(v_ready, 1)

                peeled(pe, PAIRS, pair)
                pe.wait_ge(rope, 4 * CHUNKS)
                pe.wait_ge(xT_ok, CHUNKS)
                pe.wait_ge(group_in[0], DMA * IN_DMAS)
                for k in range(IN_ONE):
                    wait(pe, wide_used, k - 1)
                    scores_for_max(pe, k % 2, 0, k)
        with ExitStack() as two:
            expT = sb(two, "expT", [P, PTN, GH, CT])
            left = sb(two, "left", [P, 2, 2 * QT])
            negs = sb(two, "negs", [P, 2, 2, 2, 3, QT], BF16)
            negT = sb(two, "negT", [2 * 3 * QT, 2, P], BF16)
            oT = sb(two, "oT", [P, 2, CT])
            rsum = sb(two, "rsum", [P, 2, NT * GH])
            att = sb(two, "att", [P, 2, NT, GH * HD])

            hi_ok = sem(two, "hi_ok")
            lo_ok = sem(two, "lo_ok")
            zeroed = sem(two, "zeroed")
            neg_in = [[sem(two, f"neg_in{r}_{f}") for f in range(2)] for r in range(RING)]
            score_ready = sem(two, "score_ready")
            exp_ok = sem(two, "exp_ok")
            masked = sem(two, "masked")
            split = sem(two, "split")
            pv_done = sem(two, "pv_done")
            oT_ok = sem(two, "oT_ok")
            recip_ok = sem(two, "recip_ok")
            att_out = [sem(two, f"att_out{h}") for h in range(2)]
            B_S, B_O = 4, 6
            NEG_DMAS = 2
            block = two.enter_context(nc.Block())

            def batches(eng, body):
                def batch(b):
                    for r in range(NG):
                        g = NG * b + r
                        body(g, b, r, wide_items(like(g)))
                peeled(eng, B, batch)

            def shifted(b, r, d):
                return b + (r + d) // NG, (r + d) % NG

            def item_of(b, r, item):
                kind, off, which = item
                bb, rr = shifted(b, r, off)
                return kind, NG * bb + rr, bb, rr, which

            @block.sync
            def _(sp):
                def load(b, r):
                    wait(sp, pv_done, NS * (NG * b + r - RING + 1))
                    load_group(sp, b, r)

                def store(b, r, half):
                    sp.dma_start(at_row(ad, b)[r, half], att[:, half]).then_inc(att_out[half], DMA)

                def place_neg(r, f):
                    for h in range(2):
                        sp.dma_start(qr[ROWS:MROWS, r, 2 * f + h, :],
                                     negT[3 * QT * h:3 * QT * (h + 1), f, :]).then_inc(neg_in[r][f], DMA)

                for f in range(2):
                    sp.wait_ge(wide_used, used_after(-1, "neg", 1, f))
                    place_neg(0, f)

                def body(g, b, r, slots):
                    if exists(g + 2, G):
                        load(*shifted(b, r, 2))
                    for item in [i for slot in slots for i in slot]:
                        kind, gg, bb, rr, which = item_of(b, r, item)
                        if kind != "max":
                            sp.wait_ge(wide_used, used_after(g, *item))
                        if kind == "out":
                            store(bb, rr, which)
                        elif kind == "neg":
                            place_neg(rr, which)

                batches(sp, body)
                sp.wait_ge(wide_used, items_before(G - 1) + 3)
                store(B - 1, NG - 1, 1)
                for half in range(2):
                    sp.wait_ge(att_out[half], DMA * G)

            @block.gpsimd
            def _(pool):
                def split_neg(g, par, f, seen):
                    wait_apart(pool, wide_used, seen, passed_pool)
                    base = 10 * g + 5 * f
                    m = mx[:, par, 2 * QT * f:2 * QT * (f + 1)]
                    n = [negs[:, par, f, :, s, :] for s in range(3)]
                    lf = left[:, f]
                    m3, l3 = (a.rearrange("p (h q) -> p h q", q=QT) for a in (m, lf))
                    nc.gpsimd.tensor_scalar(n[0], m3, -1.0, None, ALU.mult).then_inc(split, 1)
                    pool.wait_ge(split, base + 1)
                    nc.gpsimd.tensor_tensor(l3, m3, n[0], ALU.add).then_inc(split, 1)
                    wait_apart(pool, split, base + 2, passed_pool)
                    nc.gpsimd.tensor_scalar(n[1], l3, -1.0, None, ALU.mult).then_inc(split, 1)
                    pool.wait_ge(split, base + 3)
                    nc.gpsimd.tensor_tensor(l3, l3, n[1], ALU.add).then_inc(split, 1)
                    wait_apart(pool, split, base + 4, passed_pool)
                    nc.gpsimd.tensor_scalar(n[2], l3, -1.0, None, ALU.mult).then_inc(split, 1)

                for f in range(2):
                    split_neg(0, 0, f, used_after(-1, "max", 1, NM // 2 * (f + 1) - 1))

                def body(g, b, r, slots):
                    for s in range(NS):
                        if DIAGS[s]:
                            wait_apart(pool, exp_ok, GH * NS * g + GH * (s + 1), passed_pool)
                        for col in DIAGS[s]:
                            tile = expT[:, (NS * r + s) % PTN, :, col:col + P]
                            nc.gpsimd.affine_select(out=tile, in_=tile, compare_op=ALU.is_ge, fill=0.0, base=0,
                                                    pattern=[[0, GH], [1, P]], channel_multiplier=-1).then_inc(masked, 1)
                        if s in (HALF0, HALF0 + 3) and exists(g + 1, G):
                            f = int(s > HALF0)
                            split_neg(g + 1, (r + 1) % 2, f, used_after(g, "max", 1, NM // 2 * (f + 1) - 1))

                batches(pool, body)

            @block.scalar
            def _(act):
                def keep_out(g, half):
                    act.wait_ge(pv_done, NS * g + (HALF0, NS)[half])
                    if exists(g - 1, G):
                        act.wait_ge(wide_used, used_after(g, "out", -1, 1) if half else used_after(g - 1, "out", 0, 0))
                    act.activation(oT[:, half], ps[:, B_O + half], ACT.Copy).then_inc(oT_ok, 1)

                def body(g, b, r, slots):
                    for s in range(NS):
                        width = sum(n for _, _, n, _ in STEPS[s][1])
                        wait(act, pv_done, NS * g + s - PTN + 1)
                        for hh in range(GH):
                            n = GH * NS * g + GH * s + hh
                            act.wait_ge(score_ready, n + 1)
                            act.activation(expT[:, (NS * r + s) % PTN, hh, 0:width], ps[:, B_S + hh % 2, 0:width],
                                           ACT.Exp, scale=SCALE).then_inc(exp_ok, 1)
                        if s == LAG and exists(g - 1, G):
                            keep_out(g - 1, 1)
                        if s == HALF0 + LAG:
                            keep_out(g, 0)

                act.wait_ge(late_in, DMA * LATE)
                for i in range(2):
                    act.activation(w_hi[:, i], w_gu[:, i], ACT.Copy).then_inc(hi_ok, 1)
                batches(act, body)
                keep_out(G - 1, 1)

            @block.vector
            def _(dve):
                nc.vector.memset(ps[:, B_O:B_O + 2, :], 0.0).then_inc(zeroed, 1)

                def item(n, odd, kind, g, bb, rr, which):
                    dve.wait_ge(wide_ready, n + 1)
                    if kind == "max":
                        if which == 0:
                            wait(dve, split, 10 * (g - 1))
                        maxima(dve, n, odd, rr, which)
                    elif kind == "neg":
                        if exists(g - 1, G):
                            pb, pr = shifted(bb, rr, -1)
                            dve.wait_ge(neg_in[pr][which], NEG_DMAS * DMA * (pb + 1))
                        nc.vector.tensor_copy(negT[:, which, :], psw[0:6 * QT, 2 * CT * odd:2 * CT * odd + P // 2]
                                              .bitcast(BF16)).then_inc(wide_used, 1)
                    else:
                        o = ps[:, 2 * odd].rearrange("p (n w) -> p n w", w=32)
                        nc.vector.reciprocal(rsum[:, which], o[:, :, HD]).then_inc(recip_ok, 1)
                        dve.wait_ge(recip_ok, 2 * g + which + 1)
                        wait(dve, att_out[which], DMA * g)
                        nc.vector.tensor_tensor(att[:, which].rearrange("p t (h d) -> p (t h) d", d=HD), o[:, :, 0:HD],
                                                rsum[:, which].unsqueeze(2).to_broadcast([P, NT * GH, HD]),
                                                ALU.mult).then_inc(wide_used, 1)

                for k, i in list(enumerate(wide_items(-1)[0]))[IN_ONE:]:
                    item(k, k % 2, *item_of(-1, NG - 1, i))

                def body(g, b, r, slots):
                    if isinstance(g, int) and g == G - 1:
                        for i in range(2):
                            dve.wait_ge(hi_ok, i + 1)
                            nc.vector.tensor_tensor(w_lo[:, i], w_gu[:, i], w_hi[:, i], ALU.subtract).then_inc(lo_ok, 1)
                    for k, i in enumerate([i for slot in slots for i in slot]):
                        n = items_before(g) + k
                        item(n, (items_before(like(g)) + k) % 2, *item_of(b, r, i))

                batches(dve, body)
                n = items_before(G - 1) + 2
                item(n, n % 2, "out", G - 1, B - 1, NG - 1, 1)

            @block.tensor
            def _(pe):
                def item(n, odd, kind, g, bb, rr, which):
                    wait(pe, wide_used, n - 1)
                    if kind == "max":
                        if which == 0:
                            pe.wait_ge(group_in[rr], DMA * IN_DMAS * (bb + 1))
                        scores_for_max(pe, odd, rr, which)
                        return
                    elif kind == "neg":
                        wait_apart(pe, split, 10 * g + 5 * (which + 1), passed_pe)
                        last = nc.tensor.transpose(
                            psw[0:6 * QT, 2 * CT * odd:2 * CT * odd + P // 2].bitcast(BF16),
                            negs[:, rr % 2, which].rearrange("p h s q -> p (h s q)"), identb[:])
                    else:
                        pe.wait_ge(oT_ok, 2 * g + which + 1)
                        for t in range(NT):
                            last = nc.tensor.transpose(ps[:, 2 * odd, t * P:(t + 1) * P], oT[:, which, t * P:(t + 1) * P],
                                                       identf[:])
                    last.then_inc(wide_ready, 1)

                def product(g, r, s, part):
                    half, segs = STEPS[s]
                    first, end = s in (0, HALF0), s in (HALF0 - 1, NS - 1)
                    if part == 0:
                        pe.wait_ge(exp_ok, GH * NS * g + GH * (s + 1))
                        if DIAGS[s]:
                            pe.wait_ge(masked, NDIAG * g + DIAG_UNTIL[s])
                        if first:
                            wait(pe, oT_ok, 2 * (g - 1) + half + 1)
                    pieces = [(kt, q0 + o, min(CT // 2, n - o), col + o) for kt, q0, n, col in segs
                              for o in range(0, n, CT // 2)]
                    cut = (len(pieces) + 1) // 2
                    for i, (kt, q0, n, col) in list(enumerate(pieces))[slice(0, cut) if part == 0 else slice(cut, None)]:
                        at = q0 - CT * half
                        for hh in range(GH):
                            last = nc.tensor.matmul(
                                ps[32 * hh:32 * hh + VW, B_O + half, at:at + n], vr[:, r, kt, hh * VW:(hh + 1) * VW],
                                expT[:, (NS * r + s) % PTN, hh, col:col + n], start=first and i == 0,
                                stop=end and i == len(pieces) - 1)
                    if part == (len(pieces) > 1):
                        last.then_inc(pv_done, 1)

                def product_behind(g, r, s, part):
                    if s >= LAG:
                        product(g, r, s - LAG, part)
                    elif exists(g - 1, G):
                        product(g - 1, (r - 1) % NG, s - LAG + NS, part)

                for k, i in list(enumerate(wide_items(-1)[0]))[IN_ONE:]:
                    item(k, k % 2, *item_of(-1, NG - 1, i))
                pe.wait_ge(zeroed, 1)

                def body(g, b, r, slots):
                    k = 0
                    for s in range(NS):
                        for hh in range(GH):
                            n = GH * NS * g + GH * s + hh
                            if s == 0 and hh % 2 == 0:
                                pe.wait_ge(neg_in[r][hh // 2], NEG_DMAS * DMA * (b + 1))
                            wait(pe, exp_ok, n - 1)
                            for kt, q0, m, col in STEPS[s][1]:
                                last = nc.tensor.matmul(ps[:, B_S + hh % 2, col:col + m],
                                                        kr[:, r, hh, kt * P:(kt + 1) * P],
                                                        qr[:, r, hh, q0:q0 + m], start=True, stop=True)
                            last.then_inc(score_ready, 1)
                            for i in slots[GH * s + hh]:
                                item(items_before(g) + k, (items_before(like(g)) + k) % 2, *item_of(b, r, i))
                                k += 1
                            if hh % 2:
                                product_behind(g, r, s, hh // 2)

                batches(pe, body)
                for s in range(NS - LAG, NS):
                    for part in range(2):
                        product(G - 1, NG - 1, s, part)
                n = items_before(G - 1) + 2
                item(n, n % 2, "out", G - 1, B - 1, NG - 1, 1)
        mid.close()
        with ExitStack() as three:
            at3 = sb(three, "at3", [P, 2, NT, E])
            x3 = sb(three, "x3", [P, 2, NT, E])
            atT = sb(three, "atT", [P, CT])
            proj_out = sb(three, "proj_out", [P, NT, E])
            x_mid = sb(three, "x_mid", [P, 2, NT, E])
            normed = sb(three, "normed", [P, NT, E])
            xf = sb(three, "xf", [P, NT, E])
            xr = sb(three, "xr", [P, NT, E])
            xf_hi = sb(three, "xf_hi", [P, 2, CT], F32R)
            xf_lo = sb(three, "xf_lo", [P, 2, CT], F32R)
            xrT = sb(three, "xrT", [P, CT])
            st = sb(three, "st3", [P, 4, NT, 6])
            mv = sb(three, "mv3", [P, 4, NT, 2])
            ve = sb(three, "ve3", [P, 4, NT])
            rstd = sb(three, "rstd3", [P, 4, NT])
            lg = sb(three, "logits", [P, NT, NE])
            ex = sb(three, "exps", [P, NT, NE])
            pr = sb(three, "probs", [P, NT, NE])
            sc = sb(three, "scalars", [P, 9, NT])
            eq = sb(three, "equal", [P, 2, NT, NE])
            ri = sb(three, "ranked", [P, 2, NT, NE])
            oh = sb(three, "onehot", [P, 3, NT, NE])
            pm = sb(three, "unpicked", [P, NT, NE])
            pw = sb(three, "picked", [P, NT, NE])
            w_pad = sb(three, "w_pad", [P, P])
            wT = sb(three, "wT", [NT * NE, P])
            w_all = sb(three, "w_all", [P, 2, NE, CT])
            gs = sb(three, "gs", [P, 2, CT])
            hu = sb(three, "hu", [P, 4, CT])
            accT = sb(three, "accT", [P, CT])
            y = sb(three, "y", [P, NT, E])
            yo = sb(three, "yo", [P, 2, NT, E])

            chunk_in = [sem(three, f"chunk_in{p}") for p in range(2)]
            w_in3 = [sem(three, f"w_in3_{p}") for p in range(2)]
            w_out = sem(three, "w_out")
            y_out = [sem(three, f"y_out{p}") for p in range(2)]
            padded = sem(three, "padded")
            pre = sem(three, "pre")
            pre_rstd = sem(three, "pre_rstd")
            pre_pe = sem(three, "pre_pe")
            pre_act = sem(three, "pre_act")
            post = sem(three, "post")
            post_rstd = sem(three, "post_rstd")
            xf_lo_ok = sem(three, "xf_lo_ok")
            y_ready = sem(three, "y_ready")
            acc_ok = sem(three, "acc_ok")
            gate_ready = sem(three, "gate_ready")
            up_ready = sem(three, "up_ready")
            silu_ok = sem(three, "silu_ok")
            h_ok = sem(three, "h_ok")
            hw_ok = sem(three, "hw_ok")
            down = sem(three, "down")
            CHUNK_DMAS = NG + 1
            NX = NE + 1
            NH = 2 * NX
            (Y_PRE, LN_Y, X_MID, LN_X, LN_F, LG_MAX, LG_SUB, PICK) = (1, 5, 6, 10, 14, 15, 16, 36)
            K_PRE = PICK
            B_ACC, B_A, B_B, B_C = 4, 5, 6, 7
            block = three.enter_context(nc.Block())

            def steps3(eng, before, body, after):
                before()

                def pair(j):
                    for p in range(2):
                        body(2 * j + p, j, p)
                peeled(eng, PAIRS, pair)
                after()

            @block.sync
            def _(sp):
                def load(j, p):
                    c = 2 * j + p
                    wait(sp, pre, K_PRE * (c - 2) + X_MID)
                    wait(sp, pre_pe, 6 * (c - 2) + 1)
                    for hg in range(NG):
                        sp.dma_start(at3[:, p, :, hg * GH * HD:(hg + 1) * GH * HD],
                                     at_row(ad, j)[hg, p]).then_inc(chunk_in[p], DMA)
                    sp.dma_start(x3[:, p], at_row(x_v, j)[p]).then_inc(chunk_in[p], DMA)

                def spread_w(j, p):
                    c = 2 * j + p
                    sp.wait_ge(pre_act, 5 * c + 5)
                    sp.dma_start(wd[p], wT[:]).then_inc(w_out, DMA)
                    wait_apart(sp, w_out, DMA * (c + 1), passed_sp)
                    wait(sp, hw_ok, 2 * NE * (c - 1))
                    for e in range(NE):
                        sp.dma_start(w_all[:, p, e, :].rearrange("q (t n) -> q t n", n=P),
                                     wd[p].rearrange("(t e) n -> e t n", e=NE)[e].partition_broadcast(P)
                                     ).then_inc(w_in3[p], DMA)

                def store(j, p):
                    c = 2 * j + p
                    sp.wait_ge(post, 5 * c + 5)
                    sp.dma_start(at_row(out_v, j)[p], yo[:, p]).then_inc(y_out[p], DMA)

                def before():
                    load(0, 0)
                    load(0, 1)
                    spread_w(0, 0)

                def body(c, j, p):
                    if exists(c + 2, CHUNKS):
                        load(j + 1, p)
                    if exists(c - 1, CHUNKS):
                        store(j - 1 + p, 1 - p)
                    if exists(c + 1, CHUNKS):
                        spread_w(j + p, 1 - p)

                def after():
                    store(PAIRS - 1, 1)
                    for p in range(2):
                        sp.wait_ge(y_out[p], DMA * PAIRS)

                steps3(sp, before, body, after)

            @block.gpsimd
            def _(pool):
                def root(ready, count, k, done):
                    pool.wait_ge(ready, count)
                    nc.gpsimd.tensor_tensor(rstd[:, k], ve[:, k], neghalf[:], ALU.pow).then_inc(done, 1)

                def weigh(c, j, p, s):
                    for i in range(2):
                        n = NH * c + 2 * s + i
                        pool.wait_ge(h_ok, n + 1)
                        if i == 0:
                            pool.wait_ge(w_in3[p], DMA * (NE * j + NE))
                        nc.gpsimd.tensor_tensor(hu[:, (2 * s + i + 2 * p) % 4], hu[:, (2 * s + i + 2 * p) % 4],
                                                w_all[:, p, s - 1], ALU.mult).then_inc(hw_ok, 1)
                        if s == 1 and i == 0 and exists(c - 1, CHUNKS):
                            root(post, 5 * (c - 1) + 3, 3, post_rstd)

                def before():
                    for k in range(3):
                        root(pre, (4, 9, 13)[k], k, pre_rstd)

                def body(c, j, p):
                    for s in range(NX):
                        if s > 0:
                            weigh(c, j, p, s)
                        if s < 3 and exists(c + 1, CHUNKS):
                            root(pre, K_PRE * (c + 1) + (4, 9, 13)[s], s, pre_rstd)

                def after():
                    root(post, 5 * (CHUNKS - 1) + 3, 3, post_rstd)

                steps3(pool, before, body, after)

            @block.scalar
            def _(act):
                def pre_a(c):
                    act.wait_ge(pre_pe, 6 * c + 1)
                    act.activation(atT[:], ps[:, B_A], ACT.Copy).then_inc(pre_act, 1)

                def pre_b(c, p):
                    act.wait_ge(pre_pe, 6 * c + 3)
                    act.activation(xf_hi[:, p], ps[:, B_A], ACT.Copy).then_inc(pre_act, 1)
                    act.wait_ge(pre_pe, 6 * c + 4)
                    act.activation(xrT[:], ps[:, B_B], ACT.Identity, scale=cols[:, 4:5],
                                   bias=cols[:, 5:6]).then_inc(pre_act, 1)

                def pre_c(c):
                    act.wait_ge(pre, K_PRE * c + LG_SUB)
                    act.activation(ex[:], lg[:], ACT.Exp).then_inc(pre_act, 1)

                def pre_d(c):
                    act.wait_ge(pre_pe, 6 * c + 6)
                    wait(act, w_out, DMA * c)
                    act.activation(wT[:], ps[0:NT * NE, B_A, 0:P], ACT.Copy).then_inc(pre_act, 1)

                def keep_acc(c):
                    act.wait_ge(down, NH * (c + 1))
                    act.activation(accT[:], ps[:, B_ACC], ACT.Copy).then_inc(acc_ok, 1)

                def before():
                    act.wait_ge(late_in, DMA * LATE)
                    pre_a(0)
                    pre_b(0, 0)
                    pre_c(0)
                    pre_d(0)

                def body(c, j, p):
                    for s in range(NX):
                        if s == 0 and exists(c + 1, CHUNKS):
                            pre_a(c + 1)
                        for i in range(2):
                            n = NH * c + 2 * s + i
                            act.wait_ge(gate_ready, n + 1)
                            wait(act, h_ok, n - 1)
                            act.activation(gs[:, i], ps[:, 2 * i], ACT.Silu).then_inc(silu_ok, 1)
                        if s == 0 and exists(c - 1, CHUNKS):
                            keep_acc(c - 1)
                        if exists(c + 1, CHUNKS):
                            if s == 3:
                                pre_b(c + 1, 1 - p)
                            if s == 4:
                                pre_c(c + 1)
                            if s == 6:
                                pre_d(c + 1)

                steps3(act, before, body, lambda: keep_acc(CHUNKS - 1))

            @block.vector
            def _(dve):
                v = nc.vector

                def normalize(out, src, k):
                    for t in range(NT):
                        last = v.tensor_scalar(out[:, t], src[:, t], mv[:, k, t, 0:1], rstd[:, k, t:t + 1],
                                               ALU.subtract, ALU.mult)
                    return last

                def pre_a(c):
                    dve.wait_ge(pre_pe, 6 * c + 2)
                    base = K_PRE * c
                    v.tensor_tensor(proj_out[:], ps[:, B_B].rearrange("p (t e) -> p t e", e=E),
                                    bo_all[:].unsqueeze(1).to_broadcast([P, NT, E]), ALU.add).then_inc(pre, 1)
                    dve.wait_ge(pre, base + Y_PRE)
                    ln_stats(dve, pre, base + Y_PRE, proj_out[:], st[:, 0], mv[:, 0], ve[:, 0])

                def pre_b(c, j, p):
                    base = K_PRE * c
                    dve.wait_ge(pre_rstd, 3 * c + 1)
                    normalize(normed, proj_out, 0).then_inc(pre, 1)
                    dve.wait_ge(pre, base + LN_Y)
                    dve.wait_ge(chunk_in[p], DMA * CHUNK_DMAS * (j + 1))
                    v.tensor_tensor(x_mid[:, p], x3[:, p], normed[:], ALU.add).then_inc(pre, 1)
                    dve.wait_ge(pre, base + X_MID)
                    ln_stats(dve, pre, base + X_MID, x_mid[:, p], st[:, 1], mv[:, 1], ve[:, 1])

                def pre_c(c, p):
                    base = K_PRE * c
                    dve.wait_ge(pre_rstd, 3 * c + 2)
                    normalize(xf, x_mid[:, p], 1).then_inc(pre, 1)
                    dve.wait_ge(pre, base + LN_X)
                    ln_stats(dve, pre, base + LN_X, xf[:], st[:, 2], mv[:, 2], ve[:, 2])

                def pre_r(c):
                    dve.wait_ge(pre_rstd, 3 * c + 3)
                    normalize(xr, xf, 2).then_inc(pre, 1)

                def pre_lo(c, p):
                    dve.wait_ge(pre_act, 5 * c + 2)
                    v.tensor_tensor(xf_lo[:, p], ps[:, B_A], xf_hi[:, p], ALU.subtract).then_inc(xf_lo_ok, 1)

                def over(k):
                    return sc[:, k].unsqueeze(2).to_broadcast([P, NT, NE])

                def pre_d(c):
                    base = K_PRE * c
                    dve.wait_ge(pre_pe, 6 * c + 5)
                    logits = ps[:, B_C, 0:NT * NE].rearrange("p (t e) -> p t e", e=NE)
                    v.reduce_max(sc[:, 0], logits, AX_X).then_inc(pre, 1)
                    dve.wait_ge(pre, base + LG_MAX)
                    v.tensor_tensor(lg[:], logits, over(0), ALU.subtract).then_inc(pre, 1)

                def pre_e(c):
                    dve.wait_ge(pre_act, 5 * c + 4)
                    rank = rev[:].rearrange("p (t e) -> p t e", e=NE)
                    at = K_PRE * c + LG_SUB
                    ops = [
                        lambda: v.reduce_sum(sc[:, 1], ex[:], AX_X),
                        lambda: v.reciprocal(sc[:, 2], sc[:, 1]),
                        lambda: v.tensor_tensor(pr[:], ex[:], over(2), ALU.mult),
                        lambda: v.reduce_max(sc[:, 3], pr[:], AX_X),
                        lambda: v.tensor_tensor(eq[:, 0], pr[:], over(3), ALU.is_equal),
                        lambda: v.tensor_tensor(ri[:, 0], eq[:, 0], rank, ALU.mult),
                        lambda: v.reduce_max(sc[:, 4], ri[:, 0], AX_X),
                        lambda: v.tensor_tensor(oh[:, 0], ri[:, 0], over(4), ALU.is_equal),
                        lambda: v.scalar_tensor_tensor(pm[:], oh[:, 0], -2.0, pr[:], ALU.mult, ALU.add),
                        lambda: v.reduce_max(sc[:, 5], pm[:], AX_X),
                        lambda: v.tensor_tensor(eq[:, 1], pm[:], over(5), ALU.is_equal),
                        lambda: v.tensor_tensor(ri[:, 1], eq[:, 1], rank, ALU.mult),
                        lambda: v.reduce_max(sc[:, 6], ri[:, 1], AX_X),
                        lambda: v.tensor_tensor(oh[:, 1], ri[:, 1], over(6), ALU.is_equal),
                        lambda: v.tensor_tensor(oh[:, 2], oh[:, 0], oh[:, 1], ALU.add),
                        lambda: v.tensor_tensor(pw[:], pr[:], oh[:, 2], ALU.mult),
                        lambda: v.tensor_tensor(sc[:, 7], sc[:, 3], sc[:, 5], ALU.add),
                        lambda: v.tensor_scalar_add(sc[:, 7], sc[:, 7], EPS),
                        lambda: v.reciprocal(sc[:, 8], sc[:, 7]),
                        lambda: v.tensor_tensor(w_pad[:, 0:NT * NE].rearrange("p (t e) -> p t e", e=NE), pw[:], over(8),
                                                ALU.mult),
                    ]
                    assert LG_SUB + len(ops) == K_PRE
                    for k, op in enumerate(ops):
                        if k:
                            dve.wait_ge(pre, at + k)
                        op().then_inc(pre, 1)

                def post_a(c):
                    dve.wait_ge(y_ready, c + 1)
                    ln_stats(dve, post, 5 * c, ps[:, B_C].rearrange("p (t e) -> p t e", e=E), st[:, 3], mv[:, 3], ve[:, 3])

                def post_b(c, j, p):
                    dve.wait_ge(post_rstd, c + 1)
                    normalize(y, ps[:, B_C].rearrange("p (t e) -> p t e", e=E), 3).then_inc(post, 1)
                    dve.wait_ge(post, 5 * c + 4)
                    wait(dve, y_out[p], DMA * j)
                    v.tensor_tensor(yo[:, p], y[:], x_mid[:, p], ALU.add).then_inc(post, 1)

                def before():
                    v.memset(w_pad[:], 0.0).then_inc(padded, 1)
                    dve.wait_ge(padded, 1)
                    dve.wait_ge(late_in, DMA * LATE)
                    pre_a(0)
                    pre_b(0, 0, 0)
                    pre_c(0, 0)
                    pre_r(0)
                    pre_lo(0, 0)
                    pre_d(0)
                    pre_e(0)

                def body(c, j, p):
                    for s in range(NX):
                        for i in range(2):
                            n = NH * c + 2 * s + i
                            dve.wait_ge(up_ready, n + 1)
                            dve.wait_ge(silu_ok, n + 1)
                            wait(dve, down, n - 3)
                            v.tensor_tensor(hu[:, (2 * s + i + 2 * p) % 4], gs[:, i], ps[:, 2 * i + 1],
                                            ALU.mult).then_inc(h_ok, 1)
                            if s == 1 and i == 0 and exists(c - 1, CHUNKS):
                                post_a(c - 1)
                        if exists(c - 1, CHUNKS):
                            if s == 1:
                                post_b(c - 1, j - 1 + p, 1 - p)
                        if exists(c + 1, CHUNKS):
                            if s == 0:
                                pre_a(c + 1)
                            if s == 1:
                                pre_b(c + 1, j + p, 1 - p)
                            if s == 2:
                                pre_c(c + 1, 1 - p)
                            if s == 3:
                                pre_r(c + 1)
                            if s == 4:
                                pre_lo(c + 1, 1 - p)
                                pre_d(c + 1)
                            if s == 5:
                                pre_e(c + 1)

                def after():
                    post_a(CHUNKS - 1)
                    post_b(CHUNKS - 1, PAIRS - 1, 1)

                steps3(dve, before, body, after)

            @block.tensor
            def _(pe):
                def turn(bank, src, ready, count, out, tiles=NT):
                    pe.wait_ge(ready, count)
                    for t in range(tiles):
                        last = nc.tensor.transpose(ps[:, bank, t * P:(t + 1) * P], src[:, t * P:(t + 1) * P], identf[:])
                    last.then_inc(out, 1)

                def flat(a):
                    return a.rearrange("p t e -> p (t e)")

                def pre_a(c, j, p):
                    wait(pe, pre_act, 5 * c)
                    turn(B_A, flat(at3[:, p]), chunk_in[p], DMA * CHUNK_DMAS * (j + 1), pre_pe)

                def pre_b(c):
                    pe.wait_ge(pre_act, 5 * c + 1)
                    for t in range(NT):
                        last = nc.tensor.matmul(ps[:, B_B, t * P:(t + 1) * P], atT[:, t * P:(t + 1) * P], wo[:],
                                                start=True, stop=True)
                    last.then_inc(pre_pe, 1)

                def pre_c(c):
                    turn(B_A, flat(xf[:]), pre, K_PRE * c + LN_X, pre_pe)
                    turn(B_B, flat(xr[:]), pre, K_PRE * c + LN_F, pre_pe)

                def pre_d(c):
                    pe.wait_ge(pre_act, 5 * c + 3)
                    for t in range(NT):
                        last = nc.tensor.matmul(ps[:, B_C, t * NE:(t + 1) * NE], xrT[:, t * P:(t + 1) * P], gate[:],
                                                start=True, stop=True)
                    last.then_inc(pre_pe, 1)

                def pre_e(c):
                    pe.wait_ge(xf_lo_ok, c + 1)
                    turn(B_A, w_pad, pre, K_PRE * (c + 1), pre_pe, 1)

                def three_passes(out, which, e, cols_i, p):
                    nc.tensor.matmul(out, w_hi[:, which, e, cols_i], xf_hi[:, p], start=True, stop=False)
                    nc.tensor.matmul(out, w_hi[:, which, e, cols_i], xf_lo[:, p], start=False, stop=False)
                    return nc.tensor.matmul(out, w_lo[:, which, e, cols_i], xf_hi[:, p], start=False, stop=True)

                def down_product(c, p, s):
                    for i in range(2):
                        if s == 0:
                            if i == 0:
                                wait(pe, acc_ok, c)
                            pe.wait_ge(h_ok, NH * c + i + 1)
                        else:
                            pe.wait_ge(hw_ok, 2 * NE * c + 2 * (s - 1) + i + 1)
                        nc.tensor.matmul(ps[:, B_ACC], wdn[:, (s - 1) % NX, i], hu[:, (2 * s + i + 2 * p) % 4],
                                         start=s == 0 and i == 0, stop=s == NX - 1 and i == 1).then_inc(down, 1)

                def turn_y(c):
                    turn(B_C, accT, acc_ok, c + 1, y_ready)

                def before():
                    pe.wait_ge(late_in, DMA * LATE)
                    pre_a(0, 0, 0)
                    pre_b(0)
                    pre_c(0)
                    pre_d(0)
                    pre_e(0)

                def body(c, j, p):
                    for s in range(NX):
                        if s == 0 and exists(c + 1, CHUNKS):
                            pre_a(c + 1, j + p, 1 - p)
                        if s == 0:
                            pe.wait_ge(xf_lo_ok, c + 1)
                        for i in range(2):
                            n = NH * c + 2 * s + i
                            cols_i = slice(i * P, (i + 1) * P)
                            wait(pe, silu_ok, n - 1)
                            three_passes(ps[:, 2 * i], 0, (s - 1) % NX, cols_i, p).then_inc(gate_ready, 1)
                            wait(pe, h_ok, n - 1)
                            three_passes(ps[:, 2 * i + 1], 1, (s - 1) % NX, cols_i, p).then_inc(up_ready, 1)
                            if s == 1 and i == 0 and exists(c - 1, CHUNKS):
                                turn_y(c - 1)
                        if s > 0:
                            down_product(c, p, s - 1)
                        elif exists(c - 1, CHUNKS):
                            down_product(c - 1, 1 - p, NX - 1)
                        if exists(c + 1, CHUNKS):
                            if s == 0:
                                pre_b(c + 1)
                            if s == 3:
                                pre_c(c + 1)
                            if s == 4:
                                pre_d(c + 1)
                            if s == 6:
                                pre_e(c + 1)

                def after():
                    down_product(CHUNKS - 1, 1, NX - 1)
                    turn_y(CHUNKS - 1)

                steps3(pe, before, body, after)


def rotary_tables():
    inv = (np.float32(1.0) / np.float32(10000.0) ** (np.arange(0, E, 2, dtype=np.float32) / np.float32(E)))
    freqs = np.arange(S, dtype=np.float32)[:, None] * inv.astype(np.float32)[None, :]
    emb = np.concatenate([freqs, freqs], axis=-1)
    return np.cos(emb), np.sin(emb)


def kernel(**inputs):
    import concourse.bacc as bacc
    from concourse.bass_utils import run_bass_kernel_spmd

    a = {k: np.asarray(v) for k, v in inputs.items()}
    turned = (np.arange(E) + E // 2) % E
    cos, sin = rotary_tables()
    sign = np.where(np.arange(E) < E // 2, -1.0, 1.0).astype(np.float32)
    rev = np.tile(np.arange(NE, 0, -1, dtype=np.float32), NT)
    wq, bq, wk, bk = (a["L0_attn_" + n] for n in ("wqr", "bqr", "wkr", "bkr"))
    arrays = dict(
        x=a["L0_attn_x"], wq=wq, wqs=wq[:, turned], bq=np.stack([bq, bq[turned]], 1),
        wk=wk, wks=wk[:, turned], bk=np.stack([bk, bk[turned]], 1),
        wkv=a["L0_attn_wkv"], bkv=a["L0_attn_bkv"][:, None], wv=a["L0_attn_wv"], bv=a["L0_attn_bv"][None, :],
        wo=a["L0_attn_wo"], bo=a["L0_attn_bo"],
        zero=np.zeros((MROWS - ROWS, GH * S // 2), np.float32), lns=a["L0_ffn_ln_scale"][:, None], lnb=a["L0_ffn_ln_bias"][:, None],
        gate=a["L0_ffn_gate_w"].T, wg=a["L0_ffn_Wg"], wu=a["L0_ffn_Wu"], wd=a["L0_ffn_Wd"],
        swg=a["L0_ffn_sWg"], swu=a["L0_ffn_sWu"], swd=a["L0_ffn_sWd"],
        cos=cos.T, sin=(sin * sign).T, rev=rev,
    )
    nc = bacc.Bacc("TRN2", target_bir_lowering=False, num_devices=1)
    arrays = {f"in_{n}": np.ascontiguousarray(v) for n, v in arrays.items()}
    args = [nc.dram_tensor(n, v.shape, mybir.dt.from_np(v.dtype), kind="ExternalInput").ap() for n, v in arrays.items()]
    out = nc.dram_tensor("out", (B, S, E), F32, kind="ExternalOutput").ap()
    block_kernel(nc, *args, out)
    r = run_bass_kernel_spmd(nc, [arrays], core_ids=[0])
    return r.results[0]["out"]
```

```python
from contextlib import ExitStack

import numpy as np

import concourse.bass as bass
from concourse import mybir

F32 = mybir.dt.float32
F32R = mybir.dt.float32r
BF16 = mybir.dt.bfloat16
ALU = mybir.AluOpType
ACT = mybir.ActivationFunctionType
AX_X = mybir.AxisListType.X

P = 128
B, S, E = 4, 1024, 128
H, HD = 16, 8
DC = 32
NE, INTER = 8, 256
EPS = 1e-5
SCALE = HD ** -0.5
NEG = -3.0e38

CT = 512
NT = CT // P
CHUNKS = B * S // CT
PAIRS = CHUNKS // 2
GH = 4
NG = H // GH
G = B * NG
QT = S // P
VW = HD + 1
ROWS = 9 * HD
MROWS = ROWS + 3
KROWS = 96
PAIR_OF_ONES = float(np.array([0x3F803F80], np.uint32).view(np.float32)[0])
DMA = 16


def exists(i, n):
    return not isinstance(i, int) or 0 <= i < n


def wait(eng, sem, value):
    if not isinstance(value, int) or value > 0:
        eng.wait_ge(sem, value)


def wait_apart(eng, sem, value, passed):
    wait(eng, sem, value)
    if not isinstance(value, int):
        eng.sem_inc(passed, 1)


def at_row(a, b):
    if isinstance(b, int):
        return a[b]
    dims = " ".join(f"d{i}" for i in range(1, len(a.shape)))
    return a[bass.ds(b, 1)].rearrange(f"d0 {dims} -> (d0 d1) {dims[3:]}")


def peeled(eng, n, body):
    body(0)
    with eng.Fori(1, n - 1) as i:
        body(i)
    body(n - 1)


STEPS = [
    (0, [(0, 0, 512, 0)]),
    (0, [(1, 128, 384, 0), (3, 384, 128, 384)]),
    (0, [(2, 256, 256, 0)]),
    (1, [(0, 512, 512, 0)]),
    (1, [(1, 512, 512, 0)]),
    (1, [(2, 512, 512, 0)]),
    (1, [(3, 512, 512, 0)]),
    (1, [(4, 512, 512, 0)]),
    (1, [(5, 640, 384, 0), (7, 896, 128, 384)]),
    (1, [(6, 768, 256, 0)]),
]
NS = len(STEPS)
HALF0 = 3
PTN = 4
LAG = 2
DIAGS = [[col for kt, q0, n, col in segs if q0 == kt * P] for _, segs in STEPS]
DIAG_UNTIL = [sum(len(d) for d in DIAGS[:s + 1]) for s in range(NS)]
NDIAG = DIAG_UNTIL[-1]
HEAD_ITEMS = [[(7, 0)], [(3, 0), (0, CT)], [(6, 0)], [(2, 0), (1, CT)], [(5, 0)], [(4, 0)]]
MAX_ITEMS = [(hh, tiles) for hh in range(GH) for tiles in HEAD_ITEMS]
NM = len(MAX_ITEMS)
EARLY = 8
IN_ONE = 18


def wide_items(g):
    if g == -1:
        seq = [("max", 1, i) for i in range(NM)]
        return [seq[:IN_ONE + 1] + [("neg", 1, 0)] + seq[IN_ONE + 1:] + [("neg", 1, 1)]]
    nxt = [("max", 1, i) for i in range(0 if g == 0 else EARLY, NM)] if g + 1 < G else []
    neg = [("neg", 1, 0), ("neg", 1, 1)] if g + 1 < G else []
    early = [("max", 2, i) for i in range(EARLY)] if g + 2 < G else []
    prev = [("out", -1, 1)] if g > 0 else []
    if g == 0:
        seq = nxt[:17] + neg[:1] + nxt[17:22] + [("out", 0, 0)] + nxt[22:] + early[:4] + neg[1:] + early[4:]
    else:
        seq = nxt[:11] + prev + neg[:1] + nxt[11:] + early[:1] + [("out", 0, 0)] + early[1:4] + neg[1:] + early[4:]
    slots, at = [[] for _ in range(GH * NS)], 0
    for i, item in enumerate(seq):
        at = max(at, i * (GH * NS - 1) // max(N_ITEMS, len(seq)))
        if item[0] == "out":
            at = max(at, GH * (LAG + 2 + (0 if item[2] else HALF0 - 1)))
        slots[at].append(item)
    return slots


N_FIRST = NM + 2
N_ITEMS = NM + 2 + 2


def items_before(g):
    if isinstance(g, int):
        return sum((len([i for s in wide_items(k) for i in s]) for k in range(-1, g)), 0)
    return N_FIRST + EARLY - 1 + N_ITEMS * g


def like(g):
    return g if isinstance(g, int) else NG


def used_after(g, kind, off, which):
    flat = [i for slot in wide_items(like(g)) for i in slot]
    return items_before(g) + flat.index((kind, off, which)) + 1


def block_kernel(nc, x_d, wq_d, wqs_d, bq_d, wk_d, wks_d, bk_d, wkv_d, bkv_d, wv_d, bv_d, wo_d, bo_d,
                 const_d, lns_d, lnb_d, gate_d, wg_d, wu_d, wd_d, swg_d, swu_d, swd_d, cos_d, sin_d, rev_d, out_d):
    qd = nc.dram_tensor("q_parts", (B, H, 3, HD, S), BF16, kind="Internal").ap()
    kd = nc.dram_tensor("k_parts", (B, H, 3, HD, S), BF16, kind="Internal").ap()
    vd = nc.dram_tensor("v_ones", (B, P, QT, H * VW), F32, kind="Internal").ap()
    ad = nc.dram_tensor("attn", (B, NG, 2, P, NT, GH * HD), F32, kind="Internal").ap()
    wd = nc.dram_tensor("route", (2, NT * NE, P), F32, kind="Internal").ap()
    x_v = x_d.rearrange("b (h t p) e -> b h p t e", h=2, p=P)
    out_v = out_d.rearrange("b (h t p) e -> b h p t e", h=2, p=P)

    with ExitStack() as top:
        ps = top.enter_context(nc.psum_tensor("ps", [P, 8, CT], F32))
        psw = ps[:, :, :].rearrange("p b n -> p (b n)")

        def sb(stack, name, shape, dt=F32):
            return stack.enter_context(nc.sbuf_tensor(name, shape, dt))

        def sem(stack, name):
            return stack.enter_context(nc.semaphore(name))

        w_gu = sb(top, "w_gu", [P, 2, NE + 1, INTER])
        wdn = sb(top, "wdn", [P, NE + 1, 2, P])
        w_hi = sb(top, "w_hi", [P, 2, NE + 1, INTER], F32R)
        w_lo = sb(top, "w_lo", [P, 2, NE + 1, INTER], F32R)
        wo = sb(top, "wo", [P, E])
        bo_all = sb(top, "bo_all", [P, E])
        gate = sb(top, "gate", [P, NE])
        cols = sb(top, "cols", [P, 6])
        rev = sb(top, "rev", [P, NT * NE])
        identf = sb(top, "identf", [P, P])
        identb = sb(top, "identb", [P, P], BF16)
        neghalf = sb(top, "neghalf", [P, NT])
        RING = NG
        q_space = sb(top, "q_space", [P, RING, GH, S], BF16)
        qr = q_space[0:KROWS]
        kr = sb(top, "kr", [KROWS, RING, GH, S], BF16)
        vr = sb(top, "vr", [P, RING, QT, GH * VW])
        mask = sb(top, "mask", [P, S])
        x1 = sb(top, "x_in", [P, 2, NT, E])
        unread = x1[:].rearrange("p h t e -> p h (t e)").bitcast(BF16)
        mx = sb(top, "mx", [P, 2, GH * QT])
        wide_ready = sem(top, "wide_ready")
        wide_used = sem(top, "wide_used")
        IN_DMAS = 10
        group_in = [sem(top, f"group_in{r}") for r in range(RING)]
        rows_in = sem(top, "rows_in")
        mask_ok = sem(top, "mask_ok")
        late_in = sem(top, "late_in")
        ident_ok = sem(top, "ident_ok")
        passed_dve, passed_pe, passed_pool, passed_sp = (sem(top, "passed_" + n) for n in ("dve", "pe", "pool", "sp"))
        LATE = 14

        def load_group(sp, b, r):
            qg, kg = (at_row(a, b)[r * GH:(r + 1) * GH].rearrange("h s d t -> (s d) h t") for a in (qd, kd))
            for i in range(3):
                row, end = 3 * HD * i, 3 * HD * (i + 1)
                sp.dma_start(qr[row:end, r], qg).then_inc(group_in[r], DMA)
                sp.dma_start(kr[row:end - i * HD, r], kg[i * HD:]).then_inc(group_in[r], DMA)
                if i:
                    sp.dma_start(kr[end - i * HD:end, r], kg[0:i * HD]).then_inc(group_in[r], DMA)
            sp.dma_start(vr[:, r], at_row(vd, b)[:, :, r * GH * VW:(r + 1) * GH * VW]).then_inc(group_in[r], DMA)
            fill_rows(sp, qr, r, ROWS, MROWS, 0).then_inc(group_in[r], DMA)

        def fill_rows(sp, a, r, lo, hi, value):
            return sp.dma_start(a[lo:hi, r].rearrange("p h s -> p (h s)").bitcast(F32), const_d[value].partition_broadcast(hi - lo))

        def scores_for_max(pe, odd, rr, which):
            hh, tiles = MAX_ITEMS[which]
            for qi, col in tiles:
                width = P * (qi + 1)
                for lo in range(0, width, CT):
                    hi = min(width, lo + CT)
                    at = 2 * CT * odd + col
                    last = nc.tensor.matmul(psw[:, at + lo:at + hi], qr[:, rr, hh, qi * P:(qi + 1) * P],
                                            kr[:, rr, hh, lo:hi], start=True, stop=True)
            last.then_inc(wide_ready, 1)

        def maxima(dve, n, odd, rr, which):
            hh, tiles = MAX_ITEMS[which]
            wait_apart(dve, wide_used, n - 1, passed_dve)
            for qi, col in tiles:
                width = P * (qi + 1)
                last = nc.vector.tensor_tensor_reduce(
                    out=unread[:, odd, col:col + width], in0=psw[:, 2 * CT * odd + col:2 * CT * odd + col + width],
                    in1=mask[:, S - width:], scale=1.0, scalar=NEG, op0=ALU.add, op1=ALU.max,
                    accum_out=mx[:, rr % 2, QT * hh + qi:QT * hh + qi + 1])
            last.then_inc(wide_used, 1)

        def ln_stats(dve, steps, base, src, st, mv, ve):
            for t in range(NT):
                last = nc.vector.bn_stats(st[:, t, :], src[:, t, :])
            last.then_inc(steps, 1)
            wait_apart(dve, steps, base + 1, passed_dve)
            for t in range(NT):
                last = nc.vector.bn_aggr(mv[:, t, :], st[:, t, :])
            last.then_inc(steps, 1)
            dve.wait_ge(steps, base + 2)
            nc.vector.tensor_scalar_add(ve, mv[:, :, 1], EPS).then_inc(steps, 1)

        chunk_in = [sem(top, f"chunk_in{p}") for p in range(2)]
        w_out = sem(top, "w_out")
        padded = sem(top, "padded")
        pre = sem(top, "pre")
        pre_rstd = sem(top, "pre_rstd")
        pre_pe = sem(top, "pre_pe")
        pre_act = sem(top, "pre_act")
        xf_lo_ok = sem(top, "xf_lo_ok")
        CHUNK_DMAS = NG + 1
        (Y_PRE, LN_Y, X_MID, LN_X, LN_F, LG_MAX, LG_SUB, PICK) = (1, 5, 6, 10, 14, 15, 16, 36)
        K_PRE = PICK

        def pool_root(pool, c, k):
            pool.wait_ge(pre, K_PRE * c + (LN_Y - 1, LN_X - 1, LN_F - 1)[k])
            nc.gpsimd.tensor_tensor(rstd[:, k], ve[:, k], neghalf[:], ALU.pow).then_inc(pre_rstd, 1)

        def load_chunk(sp, j, p):
            for hg in range(NG):
                sp.dma_start(at3[:, p, :, hg * GH * HD:(hg + 1) * GH * HD],
                             at_row(ad, j)[hg, p]).then_inc(chunk_in[p], DMA)
            sp.dma_start(x1[:, p], at_row(x_v, j)[p]).then_inc(chunk_in[p], DMA)

        def send_w(sp, c, p):
            sp.wait_ge(pre_act, 5 * c + 5)
            sp.dma_start(wd[p], wT[:]).then_inc(w_out, DMA)

        def act_attn(act, c, bank):
            act.wait_ge(pre_pe, 6 * c + 1)
            act.activation(atT[:], ps[:, bank], ACT.Copy).then_inc(pre_act, 1)

        def act_rows(act, c, p, bank_a, bank_b):
            act.wait_ge(pre_pe, 6 * c + 3)
            act.activation(xf_hi[:, p], ps[:, bank_a], ACT.Copy).then_inc(pre_act, 1)
            act.wait_ge(pre_pe, 6 * c + 4)
            act.activation(atT[:], ps[:, bank_b], ACT.Identity, scale=cols[:, 4:5],
                           bias=cols[:, 5:6]).then_inc(pre_act, 1)

        def act_exp(act, c):
            act.wait_ge(pre, K_PRE * c + LG_SUB)
            act.activation(ex[:], lg[:], ACT.Exp).then_inc(pre_act, 1)

        def act_route(act, c, bank):
            act.wait_ge(pre_pe, 6 * c + 6)
            wait(act, w_out, DMA * c)
            act.activation(wT[:], ps[0:NT * NE, bank, 0:P], ACT.Copy).then_inc(pre_act, 1)

        def normalize(out, src, k):
            for t in range(NT):
                last = nc.vector.tensor_scalar(out[:, t], src[:, t], mv[:, k, t, 0:1], rstd[:, k, t:t + 1],
                                       ALU.subtract, ALU.mult)
            return last

        def dve_project(dve, c, bank):
            dve.wait_ge(pre_pe, 6 * c + 2)
            nc.vector.tensor_tensor(proj_out[:], ps[:, bank].rearrange("p (t e) -> p t e", e=E),
                                    bo_all[:].unsqueeze(1).to_broadcast([P, NT, E]), ALU.add).then_inc(pre, 1)

        def dve_stats(dve, c, p, k):
            base = K_PRE * c + (Y_PRE, X_MID, LN_X)[k]
            dve.wait_ge(pre, base)
            ln_stats(dve, pre, base, (proj_out[:], x_mid[:, p], xf[:])[k], st[:, k], mv[:, k], ve[:, k])

        def dve_norm(dve, c, p, k):
            dve.wait_ge(pre_rstd, 3 * c + k + 1)
            src, dst = ((proj_out[:], proj_out[:]), (x_mid[:, p], xf[:]), (xf[:], xr[:]))[k]
            normalize(dst, src, k).then_inc(pre, 1)

        def dve_mid(dve, c, j, p):
            dve.wait_ge(pre, K_PRE * c + LN_Y)
            dve.wait_ge(chunk_in[p], DMA * CHUNK_DMAS * (j + 1))
            nc.vector.tensor_tensor(x_mid[:, p], x1[:, p], proj_out[:], ALU.add).then_inc(pre, 1)

        def dve_lo(dve, c, p, bank):
            dve.wait_ge(pre_act, 5 * c + 2)
            nc.vector.tensor_tensor(xf_lo[:, p], ps[:, bank], xf_hi[:, p], ALU.subtract).then_inc(xf_lo_ok, 1)

        def over(k):
            return sc[:, k].unsqueeze(2).to_broadcast([P, NT, NE])

        def dve_logits(dve, c, bank):
            base = K_PRE * c
            dve.wait_ge(pre_pe, 6 * c + 5)
            logits = ps[:, bank, 0:NT * NE].rearrange("p (t e) -> p t e", e=NE)
            nc.vector.reduce_max(sc[:, 0], logits, AX_X).then_inc(pre, 1)
            dve.wait_ge(pre, base + LG_MAX)
            nc.vector.tensor_tensor(lg[:], logits, over(0), ALU.subtract).then_inc(pre, 1)

        def dve_route(dve, c, part, parts=3):
            if part == 0:
                dve.wait_ge(pre_act, 5 * c + 4)
            rank = rev[:].rearrange("p (t e) -> p t e", e=NE)
            at = K_PRE * c + LG_SUB
            ops = [
                lambda: nc.vector.reduce_sum(sc[:, 1], ex[:], AX_X),
                lambda: nc.vector.reciprocal(sc[:, 2], sc[:, 1]),
                lambda: nc.vector.tensor_tensor(pr[:], ex[:], over(2), ALU.mult),
                lambda: nc.vector.reduce_max(sc[:, 3], pr[:], AX_X),
                lambda: nc.vector.tensor_tensor(eq[:, 0], pr[:], over(3), ALU.is_equal),
                lambda: nc.vector.tensor_tensor(ri[:, 0], eq[:, 0], rank, ALU.mult),
                lambda: nc.vector.reduce_max(sc[:, 4], ri[:, 0], AX_X),
                lambda: nc.vector.tensor_tensor(oh[:, 0], ri[:, 0], over(4), ALU.is_equal),
                lambda: nc.vector.scalar_tensor_tensor(pm[:], oh[:, 0], -2.0, pr[:], ALU.mult, ALU.add),
                lambda: nc.vector.reduce_max(sc[:, 5], pm[:], AX_X),
                lambda: nc.vector.tensor_tensor(eq[:, 1], pm[:], over(5), ALU.is_equal),
                lambda: nc.vector.tensor_tensor(ri[:, 1], eq[:, 1], rank, ALU.mult),
                lambda: nc.vector.reduce_max(sc[:, 6], ri[:, 1], AX_X),
                lambda: nc.vector.tensor_tensor(oh[:, 1], ri[:, 1], over(6), ALU.is_equal),
                lambda: nc.vector.tensor_tensor(oh[:, 2], oh[:, 0], oh[:, 1], ALU.add),
                lambda: nc.vector.tensor_tensor(pw[:], pr[:], oh[:, 2], ALU.mult),
                lambda: nc.vector.tensor_tensor(sc[:, 7], sc[:, 3], sc[:, 5], ALU.add),
                lambda: nc.vector.tensor_scalar_add(sc[:, 7], sc[:, 7], EPS),
                lambda: nc.vector.reciprocal(sc[:, 8], sc[:, 7]),
                lambda: nc.vector.tensor_tensor(w_pad[:, 0:NT * NE].rearrange("p (t e) -> p t e", e=NE), pw[:], over(8),
                                        ALU.mult),
            ]
            assert LG_SUB + len(ops) == K_PRE
            for k in range(len(ops) * part // parts, len(ops) * (part + 1) // parts):
                if k:
                    dve.wait_ge(pre, at + k)
                ops[k]().then_inc(pre, 1)

        def turn(pe, bank, src, ready, count, out, tiles=NT):
            pe.wait_ge(ready, count)
            for t in range(tiles):
                last = nc.tensor.transpose(ps[:, bank, t * P:(t + 1) * P], src[:, t * P:(t + 1) * P], identf[:])
            last.then_inc(out, 1)

        def flat(a):
            return a.rearrange("p t e -> p (t e)")

        def pe_attn(pe, c, j, p, bank):
            wait(pe, pre_act, 5 * c)
            turn(pe, bank, flat(at3[:, p]), chunk_in[p], DMA * CHUNK_DMAS * (j + 1), pre_pe)

        def pe_project(pe, c, bank):
            pe.wait_ge(pre_act, 5 * c + 1)
            for t in range(NT):
                last = nc.tensor.matmul(ps[:, bank, t * P:(t + 1) * P], atT[:, t * P:(t + 1) * P], wo[:],
                                        start=True, stop=True)
            last.then_inc(pre_pe, 1)

        def pe_rows(pe, c, bank_a, bank_b):
            turn(pe, bank_a, flat(xf[:]), pre, K_PRE * c + LN_X, pre_pe)
            turn(pe, bank_b, flat(xr[:]), pre, K_PRE * c + LN_F, pre_pe)

        def pe_logits(pe, c, bank):
            pe.wait_ge(pre_act, 5 * c + 3)
            for t in range(NT):
                last = nc.tensor.matmul(ps[:, bank, t * NE:(t + 1) * NE], atT[:, t * P:(t + 1) * P], gate[:],
                                        start=True, stop=True)
            last.then_inc(pre_pe, 1)

        def pe_route(pe, c, bank):
            pe.wait_ge(xf_lo_ok, c + 1)
            turn(pe, bank, w_pad, pre, K_PRE * (c + 1), pre_pe, 1)

        with ExitStack() as one:
            w_q = sb(one, "w_q", [P, E])
            w_qs = sb(one, "w_qs", [P, E])
            w_k = sb(one, "w_k", [P, E])
            w_ks = sb(one, "w_ks", [P, E])
            w_kv = sb(one, "w_kv", [P, DC])
            b_kv = sb(one, "b_kv", [DC, 1])
            w_v = sb(one, "w_v", [DC + 1, E])
            cos = sb(one, "cos", [P, S])
            sin = sb(one, "sin", [P, S])
            st1 = sb(one, "st1", [P, 2, NT, 6])
            mv1 = sb(one, "mv1", [P, 2, NT, 2])
            ve1 = sb(one, "ve1", [P, 2, NT])
            rstd1 = sb(one, "rstd1", [P, 2, NT])
            xnT = sb(one, "xnT1", [P, 2, CT])
            ckvT = sb(one, "ckvT", [DC + 1, 2, CT])
            direct = sb(one, "direct", [P, 2, 2, CT])
            turned = sb(one, "turned", [P, 2, CT])
            full = sb(one, "full", [P, 2, 2, CT])
            rest = sb(one, "rest", [P, 2, 2, CT])
            parts = sb(one, "parts", [P, 2, 2, 3, CT], BF16)
            v_st = sb(one, "v_st", [P, 2, NT, H * VW])

            w_in = sem(one, "w_in")
            tables_in = sem(one, "tables_in")
            x_ok = [sem(one, f"x_in{p}") for p in range(2)]
            ones_ok = sem(one, "ones_ok")
            one_row = sem(one, "one_row")
            ln = sem(one, "ln")
            xn_ok = sem(one, "xn_ok")
            rstd_ok = sem(one, "rstd_ok")
            xT_ready = sem(one, "xT_ready")
            xT_ok = sem(one, "xT_ok")
            proj = sem(one, "proj")
            ckv_ok = sem(one, "ckv_ok")
            rope = sem(one, "rope")
            added = sem(one, "added")
            gelu_ok = sem(one, "gelu_ok")
            rest_ok = sem(one, "rest_ok")
            mid_ok = sem(one, "mid_ok")
            low_ok = sem(one, "low_ok")
            v_ready = sem(one, "v_ready")
            v_ok = sem(one, "v_ok")
            stored = [sem(one, f"stored{p}") for p in range(2)]
            NSTORE = 7
            W_DMAS = 10
            B_XT, B_C, B_V = 0, 5, 6
            block = one.enter_context(nc.Block())

            @block.sync
            def _(sp):
                sp.dma_start(x1[:, 0], x_v[0, 0]).then_inc(x_ok[0], DMA)
                for dst, src in ((cos[:], cos_d), (sin[:], sin_d)):
                    sp.dma_start(dst, src).then_inc(tables_in, DMA)
                sp.dma_start(x1[:, 1], x_v[0, 1]).then_inc(x_ok[1], DMA)
                sp.wait_ge(w_in, DMA * W_DMAS)

                def store(j, p):
                    c = 2 * j + p
                    at = slice(p * CT, (p + 1) * CT)
                    sp.wait_ge(v_ok, c + 1)
                    qb, kb, vb = at_row(qd, j), at_row(kd, j), at_row(vd, j)
                    sp.dma_start(vb[:, NT * p:NT * p + NT, :], v_st[:, p]).then_inc(stored[p], DMA)
                    sp.wait_ge(low_ok, 2 * c + 2)
                    for i in range(3):
                        for which, dst in enumerate((qb, kb)):
                            sp.dma_start(dst[:, i, :, at], parts[:, p, which, i]).then_inc(stored[p], DMA)

                def pair(j):
                    for p in range(2):
                        if not exists(j + 1, PAIRS):
                            if p == 0:
                                sp.wait_ge(rows_in, DMA * 2 * RING)
                                for i in range(2):
                                    sp.wait_ge(stored[i], DMA * NSTORE)
                            load_group(sp, 0, p)
                        if isinstance(j, int) and j == 0:
                            for r in (2 * p, 2 * p + 1):
                                fill_rows(sp, kr, r, ROWS, KROWS, 1).then_inc(rows_in, DMA)
                                fill_rows(sp, qr, r, MROWS, KROWS, 0).then_inc(rows_in, DMA)
                        if exists(2 * j + p - 1, CHUNKS):
                            store(j - 1 + p, 1 - p)

                peeled(sp, PAIRS, pair)
                store(PAIRS - 1, 1)
                for p in range(2):
                    sp.wait_ge(stored[p], DMA * NSTORE * PAIRS)

            @block.gpsimd
            def _(pool):
                nc.gpsimd.memset(neghalf[:], -0.5)
                nc.gpsimd.memset(identf[:], 0.0)
                nc.gpsimd.memset(identb[:], 0.0)
                nc.gpsimd.memset(v_st[:], 1.0).then_inc(ones_ok, 1)
                pool.wait_ge(ones_ok, 1)
                for m in (identf, identb):
                    last = nc.gpsimd.affine_select(out=m[:], in_=m[:], compare_op=ALU.not_equal, fill=1.0, base=0,
                                                   pattern=[[-1, P]], channel_multiplier=1)
                last.then_inc(ident_ok, 1)
                nc.gpsimd.memset(mask[:], 0.0).then_inc(mask_ok, 1)
                pool.wait_ge(mask_ok, 1)
                nc.gpsimd.affine_select(out=mask[:, S - P:], in_=mask[:, S - P:], compare_op=ALU.is_ge, fill=NEG, base=0,
                                        pattern=[[-1, P]], channel_multiplier=1).then_inc(mask_ok, 1)

                def root(c, p):
                    pool.wait_ge(ln, 3 * c + 3)
                    wait(pool, xn_ok, c - 1)
                    nc.gpsimd.tensor_tensor(rstd1[:, p], ve1[:, p], neghalf[:], ALU.pow).then_inc(rstd_ok, 1)

                def part_rest(c, p, i):
                    pool.wait_ge(gelu_ok, 4 * c + 2 * i + 2)
                    wait(pool, mid_ok, 2 * c - 2 + i)
                    nc.gpsimd.tensor_tensor(rest[:, p, i], full[:, p, i], parts[:, p, i, 0],
                                            ALU.subtract).then_inc(rest_ok, 1)

                def part_low(c, p, i):
                    pool.wait_ge(mid_ok, 2 * c + i + 1)
                    nc.gpsimd.tensor_tensor(parts[:, p, i, 2], rest[:, p, i], parts[:, p, i, 1],
                                            ALU.subtract).then_inc(low_ok, 1)

                root(0, 0)
                root(1, 1)

                def pair(j):
                    for p in range(2):
                        c = 2 * j + p
                        if exists(c - 1, CHUNKS):
                            part_rest(c - 1, 1 - p, 1)
                            part_low(c - 1, 1 - p, 0)
                            part_low(c - 1, 1 - p, 1)
                        if exists(c + 2, CHUNKS):
                            root(c + 2, p)
                        part_rest(c, p, 0)

                peeled(pool, PAIRS, pair)
                part_rest(CHUNKS - 1, 1, 1)
                for i in range(2):
                    part_low(CHUNKS - 1, 1, i)

            @block.scalar
            def _(act):
                for dst, src in ((w_kv[:], wkv_d), (w_q[:], wq_d), (b_kv[:], bkv_d), (cols[:, 0:2], bq_d),
                                 (w_qs[:], wqs_d), (w_k[:], wk_d), (w_ks[:], wks_d), (cols[:, 2:4], bk_d),
                                 (w_v[0:DC, :], wv_d), (w_v[DC:DC + 1, :], bv_d)):
                    act.dma_start(dst, src).then_inc(w_in, DMA)

                def keep_xT(c, p):
                    act.wait_ge(xT_ready, c + 1)
                    wait(act, proj, 5 * (c - 1))
                    act.activation(xnT[:, p], ps[:, B_XT], ACT.Copy).then_inc(xT_ok, 1)

                keep_xT(0, 0)
                act.wait_ge(w_in, DMA * W_DMAS)
                act.wait_ge(ones_ok, 1)

                def part_mid(c, p, i):
                    act.wait_ge(rest_ok, 2 * c + i + 1)
                    act.activation(parts[:, p, i, 1], rest[:, p, i], ACT.Copy).then_inc(mid_ok, 1)

                def pair(j):
                    for p in range(2):
                        c = 2 * j + p
                        if exists(j + 1, PAIRS):
                            act.wait_ge(xT_ready, c + 1)
                            act.dma_start(x1[:, p], at_row(x_v, j + 1)[p]).then_inc(x_ok[p], DMA)
                        act.wait_ge(proj, 5 * c + 1)
                        wait(act, v_ready, c - 1)
                        act.activation(ckvT[0:DC, p], ps[0:DC, B_C], ACT.Gelu, bias=b_kv[:]).then_inc(ckv_ok, 1)
                        if exists(c - 1, CHUNKS):
                            part_mid(c - 1, 1 - p, 0)
                            part_mid(c - 1, 1 - p, 1)
                        if exists(c + 1, CHUNKS):
                            keep_xT(c + 1, 1 - p)
                        wait(act, stored[p], DMA * NSTORE * j)
                        for i in range(2):
                            act.wait_ge(added, 2 * c + i + 1)
                            if i == 0:
                                wait(act, rest_ok, 2 * c - 2)
                            act.activation(full[:, p, i], direct[:, p, i], ACT.Gelu).then_inc(gelu_ok, 1)
                            act.activation(parts[:, p, i, 0], direct[:, p, i], ACT.Gelu).then_inc(gelu_ok, 1)
                            if i == 0:
                                act.wait_ge(v_ready, c + 1)
                                act.activation(v_st[:, p].rearrange("p t (h w) -> p (t h) w", w=VW)[:, :, 0:HD],
                                               ps[:, B_V].rearrange("p (th w) -> p th w", w=HD), ACT.Copy).then_inc(v_ok, 1)

                peeled(act, PAIRS, pair)
                for i in range(2):
                    part_mid(CHUNKS - 1, 1, i)

            @block.vector
            def _(dve):
                def stats(j, p):
                    c = 2 * j + p
                    dve.wait_ge(x_ok[p], DMA * (j + 1))
                    ln_stats(dve, ln, 3 * c, x1[:, p], st1[:, p], mv1[:, p], ve1[:, p])

                def normalize(c, p):
                    dve.wait_ge(rstd_ok, c + 1)
                    for t in range(NT):
                        last = nc.vector.tensor_scalar(x1[:, p, t], x1[:, p, t], mv1[:, p, t, 0:1], rstd1[:, p, t:t + 1],
                                                       ALU.subtract, ALU.mult)
                    last.then_inc(xn_ok, 1)

                nc.vector.memset(ckvT[DC:DC + 1, :, :], 1.0).then_inc(one_row, 1)
                stats(0, 0)
                normalize(0, 0)
                stats(0, 1)
                normalize(1, 1)
                dve.wait_ge(w_in, DMA * W_DMAS)
                dve.wait_ge(tables_in, DMA * 2)

                def pair(j):
                    for p in range(2):
                        c = 2 * j + p
                        at = slice(p * CT, (p + 1) * CT)
                        wait(dve, gelu_ok, 4 * c - 4)
                        for i in range(4):
                            dst, table = ((direct[:, p, i // 2], cos), (turned[:, i // 2], sin))[i % 2]
                            if i % 2:
                                wait(dve, added, 2 * c + i // 2 - 1)
                            dve.wait_ge(proj, 5 * c + 2 + i)
                            nc.vector.scalar_tensor_tensor(dst, ps[:, 1 + i], cols[:, i:i + 1],
                                                           table[:, at], ALU.add, ALU.mult).then_inc(rope, 1)
                            if i % 2:
                                dve.wait_ge(rope, 4 * c + i + 1)
                                nc.vector.tensor_tensor(direct[:, p, i // 2], direct[:, p, i // 2],
                                                        turned[:, i // 2], ALU.add).then_inc(added, 1)
                            if exists(c + 2, CHUNKS):
                                if i == 1:
                                    stats(j + 1, p)
                                if i == 3:
                                    normalize(c + 2, p)

                peeled(dve, PAIRS, pair)
                dve.wait_ge(mask_ok, 2)
                dve.wait_ge(xT_ready, CHUNKS)
                for k in range(IN_ONE):
                    dve.wait_ge(wide_ready, k + 1)
                    maxima(dve, k, k % 2, 0, k)

            @block.tensor
            def _(pe):
                def turn(c, p):
                    pe.wait_ge(xn_ok, c + 1)
                    wait(pe, xT_ok, c)
                    for t in range(NT):
                        last = nc.tensor.transpose(ps[:, B_XT, t * P:(t + 1) * P], x1[:, p, t], identf[:])
                    last.then_inc(xT_ready, 1)

                pe.wait_ge(ident_ok, 1)
                turn(0, 0)
                pe.wait_ge(w_in, DMA * W_DMAS)
                pe.wait_ge(one_row, 1)

                def pair(j):
                    for p in range(2):
                        c = 2 * j + p
                        pe.wait_ge(xT_ok, c + 1)
                        wait(pe, ckv_ok, c)
                        nc.tensor.matmul(ps[0:DC, B_C], w_kv[:], xnT[:, p], start=True, stop=True).then_inc(proj, 1)
                        for i, w in enumerate((w_q, w_qs, w_k, w_ks)):
                            wait(pe, rope, 4 * (c - 1) + 1 + i)
                            nc.tensor.matmul(ps[:, 1 + i], w[:], xnT[:, p], start=True, stop=True).then_inc(proj, 1)
                            if i == 1 and exists(c + 1, CHUNKS):
                                turn(c + 1, 1 - p)
                        pe.wait_ge(ckv_ok, c + 1)
                        wait(pe, v_ok, c)
                        for t in range(NT):
                            last = nc.tensor.matmul(ps[:, B_V, t * P:(t + 1) * P], ckvT[:, p, t * P:(t + 1) * P],
                                                    w_v[:], start=True, stop=True)
                        last.then_inc(v_ready, 1)

                peeled(pe, PAIRS, pair)
                pe.wait_ge(rope, 4 * CHUNKS)
                pe.wait_ge(xT_ok, CHUNKS)
                pe.wait_ge(group_in[0], DMA * IN_DMAS)
                for k in range(IN_ONE):
                    wait(pe, wide_used, k - 1)
                    scores_for_max(pe, k % 2, 0, k)
        at3 = sb(top, "at3", [P, 2, NT, E])
        atT = sb(top, "atT", [P, CT])
        proj_out = sb(top, "proj_out", [P, NT, E])
        x_mid = sb(top, "x_mid", [P, 2, NT, E])
        xf = sb(top, "xf", [P, NT, E])
        xr = sb(top, "xr", [P, NT, E])
        xf_hi = sb(top, "xf_hi", [P, 2, CT], F32R)
        xf_lo = sb(top, "xf_lo", [P, 2, CT], F32R)
        st = sb(top, "st3", [P, 4, NT, 6])
        mv = sb(top, "mv3", [P, 4, NT, 2])
        ve = sb(top, "ve3", [P, 4, NT])
        rstd = sb(top, "rstd3", [P, 4, NT])
        lg = sb(top, "logits", [P, NT, NE])
        ex = sb(top, "exps", [P, NT, NE])
        pr = sb(top, "probs", [P, NT, NE])
        sc = sb(top, "scalars", [P, 9, NT])
        eq = sb(top, "equal", [P, 2, NT, NE])
        ri = sb(top, "ranked", [P, 2, NT, NE])
        oh = sb(top, "onehot", [P, 3, NT, NE])
        pm = sb(top, "unpicked", [P, NT, NE])
        pw = sb(top, "picked", [P, NT, NE])
        w_pad = sb(top, "w_pad", [P, P])
        wT = sb(top, "wT", [NT * NE, P])
        with ExitStack() as two:
            expT = sb(two, "expT", [P, PTN, GH, CT])
            left = sb(two, "left", [P, 2, 2 * QT])
            negs = sb(two, "negs", [P, 2, 2, 2, 3, QT], BF16)
            negT = sb(two, "negT", [2 * 3 * QT, 2, P], BF16)
            oT = sb(two, "oT", [P, 2, CT])
            rsum = sb(two, "rsum", [P, 2, NT * GH])
            att = sb(two, "att", [P, 2, NT, GH * HD])

            hi_ok = sem(two, "hi_ok")
            lo_ok = sem(two, "lo_ok")
            zeroed = sem(two, "zeroed")
            neg_in = [[sem(two, f"neg_in{r}_{f}") for f in range(2)] for r in range(RING)]
            score_ready = sem(two, "score_ready")
            exp_ok = sem(two, "exp_ok")
            masked = sem(two, "masked")
            split = sem(two, "split")
            pv_done = sem(two, "pv_done")
            oT_ok = sem(two, "oT_ok")
            recip_ok = sem(two, "recip_ok")
            att_out = [sem(two, f"att_out{h}") for h in range(2)]
            B_S, B_O = 4, 6
            NEG_DMAS = 2
            block = two.enter_context(nc.Block())

            def batches(eng, body):
                def batch(b):
                    for r in range(NG):
                        g = NG * b + r
                        body(g, b, r, wide_items(like(g)))
                peeled(eng, B, batch)

            def shifted(b, r, d):
                return b + (r + d) // NG, (r + d) % NG

            def item_of(b, r, item):
                kind, off, which = item
                bb, rr = shifted(b, r, off)
                return kind, NG * bb + rr, bb, rr, which

            def last_group(g):
                return isinstance(g, int) and g == G - 1

            B_A, B_B = 1, 3

            @block.sync
            def _(sp):
                def load(b, r):
                    wait(sp, pv_done, NS * (NG * b + r - RING + 1))
                    load_group(sp, b, r)

                def store(b, r, half):
                    sp.dma_start(at_row(ad, b)[r, half], att[:, half]).then_inc(att_out[half], DMA)

                def place_neg(r, f):
                    for h in range(2):
                        sp.dma_start(qr[ROWS:MROWS, r, 2 * f + h, :],
                                     negT[3 * QT * h:3 * QT * (h + 1), f, :]).then_inc(neg_in[r][f], DMA)

                for f in range(2):
                    sp.wait_ge(wide_used, used_after(-1, "neg", 1, f))
                    place_neg(0, f)
                for dst, src in ((wo[:], wo_d), (bo_all[:], bo_d.partition_broadcast(P)), (gate[:], gate_d),
                                 (cols[:, 4:5], lns_d), (cols[:, 5:6], lnb_d), (rev[:], rev_d.partition_broadcast(P)),
                                 (w_gu[:, 0, 0:NE, :], wg_d.rearrange("e h i -> h e i")),
                                 (w_gu[:, 1, 0:NE, :], wu_d.rearrange("e h i -> h e i")),
                                 (w_gu[:, 0, NE, :], swg_d), (w_gu[:, 1, NE, :], swu_d)):
                    sp.dma_start(dst, src).then_inc(late_in, DMA)
                for i in range(2):
                    rows = slice(P * i, P * (i + 1))
                    sp.dma_start(wdn[:, 0:NE, i, :], wd_d[:, rows, :].rearrange("e k h -> k e h")).then_inc(late_in, DMA)
                    sp.dma_start(wdn[:, NE, i, :], swd_d[rows, :]).then_inc(late_in, DMA)

                def body(g, b, r, slots):
                    if exists(g + 2, G):
                        load(*shifted(b, r, 2))
                    if last_group(g):
                        for half in range(2):
                            sp.wait_ge(att_out[half], DMA * NG)
                        sp.wait_ge(wide_used, items_before(G - 1))
                        for p in range(2):
                            load_chunk(sp, 0, p)
                    for item in [i for slot in slots for i in slot]:
                        kind, gg, bb, rr, which = item_of(b, r, item)
                        if kind != "max":
                            sp.wait_ge(wide_used, used_after(g, *item))
                        if kind == "out":
                            store(bb, rr, which)
                        elif kind == "neg":
                            place_neg(rr, which)

                batches(sp, body)
                sp.wait_ge(wide_used, items_before(G - 1) + 3)
                store(B - 1, NG - 1, 1)
                send_w(sp, 0, 0)
                for half in range(2):
                    sp.wait_ge(att_out[half], DMA * G)

            @block.gpsimd
            def _(pool):
                def split_neg(g, par, f, seen):
                    wait_apart(pool, wide_used, seen, passed_pool)
                    base = 10 * g + 5 * f
                    m = mx[:, par, 2 * QT * f:2 * QT * (f + 1)]
                    n = [negs[:, par, f, :, s, :] for s in range(3)]
                    lf = left[:, f]
                    m3, l3 = (a.rearrange("p (h q) -> p h q", q=QT) for a in (m, lf))
                    nc.gpsimd.tensor_scalar(n[0], m3, -1.0, None, ALU.mult).then_inc(split, 1)
                    pool.wait_ge(split, base + 1)
                    nc.gpsimd.tensor_tensor(l3, m3, n[0], ALU.add).then_inc(split, 1)
                    wait_apart(pool, split, base + 2, passed_pool)
                    nc.gpsimd.tensor_scalar(n[1], l3, -1.0, None, ALU.mult).then_inc(split, 1)
                    pool.wait_ge(split, base + 3)
                    nc.gpsimd.tensor_tensor(l3, l3, n[1], ALU.add).then_inc(split, 1)
                    wait_apart(pool, split, base + 4, passed_pool)
                    nc.gpsimd.tensor_scalar(n[2], l3, -1.0, None, ALU.mult).then_inc(split, 1)

                for f in range(2):
                    split_neg(0, 0, f, used_after(-1, "max", 1, NM // 2 * (f + 1) - 1))

                def body(g, b, r, slots):
                    for s in range(NS):
                        if DIAGS[s]:
                            wait_apart(pool, exp_ok, GH * NS * g + GH * (s + 1), passed_pool)
                        for col in DIAGS[s]:
                            tile = expT[:, (NS * r + s) % PTN, :, col:col + P]
                            nc.gpsimd.affine_select(out=tile, in_=tile, compare_op=ALU.is_ge, fill=0.0, base=0,
                                                    pattern=[[0, GH], [1, P]], channel_multiplier=-1).then_inc(masked, 1)
                        if last_group(g) and HALF0 <= s < HALF0 + 3:
                            pool_root(pool, 0, s - HALF0)
                        if s in (HALF0, HALF0 + 3) and exists(g + 1, G):
                            f = int(s > HALF0)
                            split_neg(g + 1, (r + 1) % 2, f, used_after(g, "max", 1, NM // 2 * (f + 1) - 1))

                batches(pool, body)

            @block.scalar
            def _(act):
                def keep_out(g, half):
                    act.wait_ge(pv_done, NS * g + (HALF0, NS)[half])
                    if exists(g - 1, G):
                        act.wait_ge(wide_used, used_after(g, "out", -1, 1) if half else used_after(g - 1, "out", 0, 0))
                    act.activation(oT[:, half], ps[:, B_O + half], ACT.Copy).then_inc(oT_ok, 1)

                def body(g, b, r, slots):
                    for s in range(NS):
                        width = sum(n for _, _, n, _ in STEPS[s][1])
                        wait(act, pv_done, NS * g + s - PTN + 1)
                        for hh in range(GH):
                            n = GH * NS * g + GH * s + hh
                            act.wait_ge(score_ready, n + 1)
                            act.activation(expT[:, (NS * r + s) % PTN, hh, 0:width], ps[:, B_S + hh % 2, 0:width],
                                           ACT.Exp, scale=SCALE).then_inc(exp_ok, 1)
                        if s == LAG and exists(g - 1, G):
                            keep_out(g - 1, 1)
                        if s == HALF0 + LAG:
                            keep_out(g, 0)
                        if last_group(g):
                            if s == 1:
                                act.wait_ge(late_in, DMA * LATE)
                                act_attn(act, 0, B_A)
                            if s == 7:
                                act_rows(act, 0, 0, B_A, B_B)
                            if s == 8:
                                act_exp(act, 0)

                batches(act, body)
                keep_out(G - 1, 1)
                act_route(act, 0, B_A)

            @block.vector
            def _(dve):
                nc.vector.memset(ps[:, B_O:B_O + 2, :], 0.0).then_inc(zeroed, 1)
                nc.vector.memset(w_pad[:], 0.0).then_inc(padded, 1)
                dve.wait_ge(padded, 1)

                def item(n, odd, kind, g, bb, rr, which):
                    dve.wait_ge(wide_ready, n + 1)
                    if kind == "max":
                        if which == 0:
                            wait(dve, split, 10 * (g - 1))
                        maxima(dve, n, odd, rr, which)
                    elif kind == "neg":
                        if exists(g - 1, G):
                            pb, pr = shifted(bb, rr, -1)
                            dve.wait_ge(neg_in[pr][which], NEG_DMAS * DMA * (pb + 1))
                        nc.vector.tensor_copy(negT[:, which, :], psw[0:6 * QT, 2 * CT * odd:2 * CT * odd + P // 2]
                                              .bitcast(BF16)).then_inc(wide_used, 1)
                    else:
                        o = ps[:, 2 * odd].rearrange("p (n w) -> p n w", w=32)
                        nc.vector.reciprocal(rsum[:, which], o[:, :, HD]).then_inc(recip_ok, 1)
                        dve.wait_ge(recip_ok, 2 * g + which + 1)
                        wait(dve, att_out[which], DMA * g)
                        nc.vector.tensor_tensor(att[:, which].rearrange("p t (h d) -> p (t h) d", d=HD), o[:, :, 0:HD],
                                                rsum[:, which].unsqueeze(2).to_broadcast([P, NT * GH, HD]),
                                                ALU.mult).then_inc(wide_used, 1)

                for k, i in list(enumerate(wide_items(-1)[0]))[IN_ONE:]:
                    item(k, k % 2, *item_of(-1, NG - 1, i))

                def body(g, b, r, slots):
                    if last_group(g):
                        dve.wait_ge(late_in, DMA * LATE)
                        for i in range(2):
                            nc.vector.tensor_copy(w_hi[:, i], w_gu[:, i]).then_inc(hi_ok, 1)
                            dve.wait_ge(hi_ok, i + 1)
                            nc.vector.tensor_tensor(w_lo[:, i], w_gu[:, i], w_hi[:, i], ALU.subtract).then_inc(lo_ok, 1)
                    if last_group(g):
                        dve_project(dve, 0, B_B)
                        for m in range(3):
                            dve_stats(dve, 0, 0, m)
                            dve_norm(dve, 0, 0, m)
                            if m == 0:
                                dve_mid(dve, 0, 0, 0)
                    for k, i in enumerate([i for slot in slots for i in slot]):
                        n = items_before(g) + k
                        item(n, (items_before(like(g)) + k) % 2, *item_of(b, r, i))
                    if last_group(g):
                        dve_lo(dve, 0, 0, B_A)
                        dve_logits(dve, 0, B_B)
                        for part in range(3):
                            dve_route(dve, 0, part)

                batches(dve, body)
                n = items_before(G - 1) + 2
                item(n, n % 2, "out", G - 1, B - 1, NG - 1, 1)

            @block.tensor
            def _(pe):
                def item(n, odd, kind, g, bb, rr, which):
                    wait(pe, wide_used, n - 1)
                    if kind == "max":
                        if which == 0:
                            pe.wait_ge(group_in[rr], DMA * IN_DMAS * (bb + 1))
                        scores_for_max(pe, odd, rr, which)
                        return
                    elif kind == "neg":
                        wait_apart(pe, split, 10 * g + 5 * (which + 1), passed_pe)
                        last = nc.tensor.transpose(
                            psw[0:6 * QT, 2 * CT * odd:2 * CT * odd + P // 2].bitcast(BF16),
                            negs[:, rr % 2, which].rearrange("p h s q -> p (h s q)"), identb[:])
                    else:
                        pe.wait_ge(oT_ok, 2 * g + which + 1)
                        for t in range(NT):
                            last = nc.tensor.transpose(ps[:, 2 * odd, t * P:(t + 1) * P], oT[:, which, t * P:(t + 1) * P],
                                                       identf[:])
                    last.then_inc(wide_ready, 1)

                def product(g, r, s, part):
                    half, segs = STEPS[s]
                    first, end = s in (0, HALF0), s in (HALF0 - 1, NS - 1)
                    if part == 0:
                        pe.wait_ge(exp_ok, GH * NS * g + GH * (s + 1))
                        if DIAGS[s]:
                            pe.wait_ge(masked, NDIAG * g + DIAG_UNTIL[s])
                        if first:
                            wait(pe, oT_ok, 2 * (g - 1) + half + 1)
                    pieces = [(kt, q0 + o, min(CT // 2, n - o), col + o) for kt, q0, n, col in segs
                              for o in range(0, n, CT // 2)]
                    cut = (len(pieces) + 1) // 2
                    for i, (kt, q0, n, col) in list(enumerate(pieces))[slice(0, cut) if part == 0 else slice(cut, None)]:
                        at = q0 - CT * half
                        for hh in range(GH):
                            last = nc.tensor.matmul(
                                ps[32 * hh:32 * hh + VW, B_O + half, at:at + n], vr[:, r, kt, hh * VW:(hh + 1) * VW],
                                expT[:, (NS * r + s) % PTN, hh, col:col + n], start=first and i == 0,
                                stop=end and i == len(pieces) - 1)
                    if part == (len(pieces) > 1):
                        last.then_inc(pv_done, 1)

                def product_behind(g, r, s, part):
                    if s >= LAG:
                        product(g, r, s - LAG, part)
                    elif exists(g - 1, G):
                        product(g - 1, (r - 1) % NG, s - LAG + NS, part)

                for k, i in list(enumerate(wide_items(-1)[0]))[IN_ONE:]:
                    item(k, k % 2, *item_of(-1, NG - 1, i))
                pe.wait_ge(zeroed, 1)

                def body(g, b, r, slots):
                    k = 0
                    for s in range(NS):
                        for hh in range(GH):
                            n = GH * NS * g + GH * s + hh
                            if s == 0 and hh % 2 == 0:
                                pe.wait_ge(neg_in[r][hh // 2], NEG_DMAS * DMA * (b + 1))
                            wait(pe, exp_ok, n - 1)
                            for kt, q0, m, col in STEPS[s][1]:
                                last = nc.tensor.matmul(ps[:, B_S + hh % 2, col:col + m],
                                                        kr[:, r, hh, kt * P:(kt + 1) * P],
                                                        qr[:, r, hh, q0:q0 + m], start=True, stop=True)
                            last.then_inc(score_ready, 1)
                            for i in slots[GH * s + hh]:
                                item(items_before(g) + k, (items_before(like(g)) + k) % 2, *item_of(b, r, i))
                                k += 1
                            if hh % 2:
                                product_behind(g, r, s, hh // 2)
                        if last_group(g):
                            if s == 0:
                                pe.wait_ge(late_in, DMA * LATE)
                                pe_attn(pe, 0, 0, 0, B_A)
                            if s == 1:
                                pe_project(pe, 0, B_B)
                            if s == 7:
                                pe_rows(pe, 0, B_A, B_B)
                                pe_logits(pe, 0, B_B)

                batches(pe, body)
                for s in range(NS - LAG, NS):
                    for part in range(2):
                        product(G - 1, NG - 1, s, part)
                n = items_before(G - 1) + 2
                pe_route(pe, 0, B_A)
                item(n, n % 2, "out", G - 1, B - 1, NG - 1, 1)
        with ExitStack() as three:
            w_all = q_space[:].rearrange("p r h s -> p (r h s)").bitcast(F32).rearrange("p (c e n) -> p c e n", c=2, e=NE)
            gs = sb(three, "gs", [P, 2, CT])
            hu = sb(three, "hu", [P, 4, CT])
            accT = sb(three, "accT", [P, CT])
            y = sb(three, "y", [P, NT, E])
            yo = sb(three, "yo", [P, 2, NT, E])

            w_in3 = [sem(three, f"w_in3_{p}") for p in range(2)]
            y_out = [sem(three, f"y_out{p}") for p in range(2)]
            post = sem(three, "post")
            post_rstd = sem(three, "post_rstd")
            y_ready = sem(three, "y_ready")
            acc_ok = sem(three, "acc_ok")
            gate_ready = sem(three, "gate_ready")
            up_ready = sem(three, "up_ready")
            silu_ok = sem(three, "silu_ok")
            h_ok = sem(three, "h_ok")
            hw_ok = sem(three, "hw_ok")
            down = sem(three, "down")
            NX = NE + 1
            NH = 2 * NX
            B_ACC, B_A, B_B, B_C = 4, 5, 6, 7
            block = three.enter_context(nc.Block())

            def steps3(body, after, eng):
                def pair(j):
                    for p in range(2):
                        body(2 * j + p, j, p)
                peeled(eng, PAIRS, pair)
                after()

            @block.sync
            def _(sp):
                def load(j, p):
                    c = 2 * j + p
                    wait(sp, pre, K_PRE * (c - 2) + X_MID)
                    wait(sp, pre_pe, 6 * (c - 2) + 1)
                    load_chunk(sp, j, p)

                def spread_w(j, p):
                    c = 2 * j + p
                    wait_apart(sp, w_out, DMA * (c + 1), passed_sp)
                    wait(sp, hw_ok, 2 * NE * (c - 1))
                    for e in range(NE):
                        sp.dma_start(w_all[:, p, e, :].rearrange("q (t n) -> q t n", n=P),
                                     wd[p].rearrange("(t e) n -> e t n", e=NE)[e].partition_broadcast(P)
                                     ).then_inc(w_in3[p], DMA)

                def store(j, p):
                    c = 2 * j + p
                    sp.wait_ge(post, 5 * c + 5)
                    sp.dma_start(at_row(out_v, j)[p], yo[:, p]).then_inc(y_out[p], DMA)

                def before():
                    spread_w(0, 0)

                def body(c, j, p):
                    if exists(c + 2, CHUNKS):
                        load(j + 1, p)
                    if exists(c - 1, CHUNKS):
                        store(j - 1 + p, 1 - p)
                    if exists(c + 1, CHUNKS):
                        send_w(sp, c + 1, 1 - p)
                        spread_w(j + p, 1 - p)

                def after():
                    store(PAIRS - 1, 1)
                    for p in range(2):
                        sp.wait_ge(y_out[p], DMA * PAIRS)

                before()
                steps3(body, after, sp)

            @block.gpsimd
            def _(pool):
                def weigh(c, j, p, s):
                    for i in range(2):
                        n = NH * c + 2 * s + i
                        pool.wait_ge(h_ok, n + 1)
                        if i == 0:
                            pool.wait_ge(w_in3[p], DMA * (NE * j + NE))
                        nc.gpsimd.tensor_tensor(hu[:, (2 * s + i + 2 * p) % 4], hu[:, (2 * s + i + 2 * p) % 4],
                                                w_all[:, p, s - 1], ALU.mult).then_inc(hw_ok, 1)
                        if i == 0:
                            if s == 1 and exists(c - 1, CHUNKS):
                                root_y(c - 1)
                            if s in (2, 3, 4) and exists(c + 1, CHUNKS):
                                pool_root(pool, c + 1, s - 2)

                def root_y(c):
                    pool.wait_ge(post, 5 * c + 3)
                    nc.gpsimd.tensor_tensor(rstd[:, 3], ve[:, 3], neghalf[:], ALU.pow).then_inc(post_rstd, 1)

                def body(c, j, p):
                    for s in range(1, NX):
                        weigh(c, j, p, s)

                def after():
                    root_y(CHUNKS - 1)

                steps3(body, after, pool)

            @block.scalar
            def _(act):
                def keep_acc(c):
                    act.wait_ge(down, NH * (c + 1))
                    act.activation(accT[:], ps[:, B_ACC], ACT.Copy).then_inc(acc_ok, 1)

                def body(c, j, p):
                    for s in range(NX):
                        if s == 0 and exists(c + 1, CHUNKS):
                            act_attn(act, c + 1, B_A)
                        for i in range(2):
                            n = NH * c + 2 * s + i
                            if s == 6 and i == 1 and exists(c + 1, CHUNKS):
                                act_exp(act, c + 1)
                            act.wait_ge(gate_ready, n + 1)
                            wait(act, h_ok, n - 1)
                            act.activation(gs[:, i], ps[:, 2 * i], ACT.Silu).then_inc(silu_ok, 1)
                            if i == 0 and exists(c + 1, CHUNKS):
                                if s == 5:
                                    act_rows(act, c + 1, 1 - p, B_A, B_B)
                                if s == 8:
                                    act_route(act, c + 1, B_A)
                        if s == 0 and exists(c - 1, CHUNKS):
                            keep_acc(c - 1)

                def after():
                    keep_acc(CHUNKS - 1)

                steps3(body, after, act)

            @block.vector
            def _(dve):
                v = nc.vector

                def post_a(c):
                    dve.wait_ge(y_ready, c + 1)
                    ln_stats(dve, post, 5 * c, ps[:, B_C].rearrange("p (t e) -> p t e", e=E), st[:, 3], mv[:, 3], ve[:, 3])

                def post_norm(c):
                    dve.wait_ge(post_rstd, c + 1)
                    normalize(y, ps[:, B_C].rearrange("p (t e) -> p t e", e=E), 3).then_inc(post, 1)

                def post_add(c, j, p):
                    dve.wait_ge(post, 5 * c + 4)
                    wait(dve, y_out[p], DMA * j)
                    v.tensor_tensor(yo[:, p], y[:], x_mid[:, p], ALU.add).then_inc(post, 1)

                def beside(c, j, p, at):
                    if exists(c - 1, CHUNKS):
                        if at == 2:
                            post_a(c - 1)
                        if at == 3:
                            post_norm(c - 1)
                        if at == 4:
                            post_add(c - 1, j - 1 + p, 1 - p)
                    if exists(c + 1, CHUNKS):
                        if at == 1:
                            dve_project(dve, c + 1, B_B)
                        if at == 4:
                            dve_stats(dve, c + 1, 1 - p, 0)
                        if at == 5:
                            dve_norm(dve, c + 1, 1 - p, 0)
                        if at == 6:
                            dve_mid(dve, c + 1, j + p, 1 - p)
                            dve_stats(dve, c + 1, 1 - p, 1)
                        if at == 7:
                            dve_norm(dve, c + 1, 1 - p, 1)
                        if at == 8:
                            dve_stats(dve, c + 1, 1 - p, 2)
                        if at == 9:
                            dve_norm(dve, c + 1, 1 - p, 2)
                        if at == 11:
                            dve_lo(dve, c + 1, 1 - p, B_A)
                        if at == 12:
                            dve_logits(dve, c + 1, B_C)
                        if at in (13, 14, 15):
                            dve_route(dve, c + 1, at - 13)

                def body(c, j, p):
                    for s in range(NX):
                        for i in range(2):
                            n = NH * c + 2 * s + i
                            dve.wait_ge(up_ready, n + 1)
                            dve.wait_ge(silu_ok, n + 1)
                            wait(dve, down, n - 3)
                            v.tensor_tensor(hu[:, (2 * s + i + 2 * p) % 4], gs[:, i], ps[:, 2 * i + 1],
                                            ALU.mult).then_inc(h_ok, 1)
                            beside(c, j, p, 2 * s + i)

                def after():
                    post_a(CHUNKS - 1)
                    post_norm(CHUNKS - 1)
                    post_add(CHUNKS - 1, PAIRS - 1, 1)

                steps3(body, after, dve)

            @block.tensor
            def _(pe):
                def three_passes(out, which, e, cols_i, p):
                    nc.tensor.matmul(out, w_hi[:, which, e, cols_i], xf_hi[:, p], start=True, stop=False)
                    nc.tensor.matmul(out, w_hi[:, which, e, cols_i], xf_lo[:, p], start=False, stop=False)
                    return nc.tensor.matmul(out, w_lo[:, which, e, cols_i], xf_hi[:, p], start=False, stop=True)

                def down_product(c, p, s, i):
                    first, last = (s, i) == (0, 0), (s, i) == (NX - 1, 1)
                    if first:
                        wait(pe, acc_ok, c)
                    if s == 0:
                        pe.wait_ge(h_ok, NH * c + i + 1)
                    else:
                        pe.wait_ge(hw_ok, 2 * NE * c + 2 * (s - 1) + i + 1)
                    nc.tensor.matmul(ps[:, B_ACC], wdn[:, (s - 1) % NX, i], hu[:, (2 * s + i + 2 * p) % 4],
                                     start=first, stop=last).then_inc(down, 1)

                def turn_y(c):
                    turn(pe, B_C, accT, acc_ok, c + 1, y_ready)

                def body(c, j, p):
                    for s in range(NX):
                        if s == 0 and exists(c + 1, CHUNKS):
                            pe_attn(pe, c + 1, j + p, 1 - p, B_A)
                        if s == 0:
                            pe.wait_ge(xf_lo_ok, c + 1)
                        for i in range(2):
                            n = NH * c + 2 * s + i
                            cols_i = slice(i * P, (i + 1) * P)
                            wait(pe, silu_ok, n - 1)
                            three_passes(ps[:, 2 * i], 0, (s - 1) % NX, cols_i, p).then_inc(gate_ready, 1)
                            wait(pe, h_ok, n - 1)
                            three_passes(ps[:, 2 * i + 1], 1, (s - 1) % NX, cols_i, p).then_inc(up_ready, 1)
                            if s == 1 and i == 0 and exists(c - 1, CHUNKS):
                                turn_y(c - 1)
                            if s > 0:
                                down_product(c, p, s - 1, i)
                            elif exists(c - 1, CHUNKS):
                                down_product(c - 1, 1 - p, NX - 1, i)
                            if exists(c + 1, CHUNKS):
                                if 2 * s + i == 0:
                                    pe_project(pe, c + 1, B_B)
                                if 2 * s + i == 10:
                                    pe_rows(pe, c + 1, B_A, B_B)
                                if 2 * s + i == 11:
                                    pe_logits(pe, c + 1, B_C)
                                if 2 * s + i == 16:
                                    pe_route(pe, c + 1, B_A)

                def after():
                    for i in range(2):
                        down_product(CHUNKS - 1, 1, NX - 1, i)
                    turn_y(CHUNKS - 1)

                steps3(body, after, pe)


def rotary_tables():
    inv = (np.float32(1.0) / np.float32(10000.0) ** (np.arange(0, E, 2, dtype=np.float32) / np.float32(E)))
    freqs = np.arange(S, dtype=np.float32)[:, None] * inv.astype(np.float32)[None, :]
    emb = np.concatenate([freqs, freqs], axis=-1)
    return np.cos(emb), np.sin(emb)


def kernel(**inputs):
    import concourse.bacc as bacc
    from concourse.bass_utils import run_bass_kernel_spmd

    a = {k: np.asarray(v) for k, v in inputs.items()}
    turned = (np.arange(E) + E // 2) % E
    cos, sin = rotary_tables()
    sign = np.where(np.arange(E) < E // 2, -1.0, 1.0).astype(np.float32)
    rev = np.tile(np.arange(NE, 0, -1, dtype=np.float32), NT)
    wq, bq, wk, bk = (a["L0_attn_" + n] for n in ("wqr", "bqr", "wkr", "bkr"))
    arrays = dict(
        x=a["L0_attn_x"], wq=wq, wqs=wq[:, turned], bq=np.stack([bq, bq[turned]], 1),
        wk=wk, wks=wk[:, turned], bk=np.stack([bk, bk[turned]], 1),
        wkv=a["L0_attn_wkv"], bkv=a["L0_attn_bkv"][:, None], wv=a["L0_attn_wv"], bv=a["L0_attn_bv"][None, :],
        wo=a["L0_attn_wo"], bo=a["L0_attn_bo"],
        const=np.repeat(np.array([[0.0], [PAIR_OF_ONES]], np.float32), GH * S // 2, axis=1), lns=a["L0_ffn_ln_scale"][:, None], lnb=a["L0_ffn_ln_bias"][:, None],
        gate=a["L0_ffn_gate_w"].T, wg=a["L0_ffn_Wg"], wu=a["L0_ffn_Wu"], wd=a["L0_ffn_Wd"],
        swg=a["L0_ffn_sWg"], swu=a["L0_ffn_sWu"], swd=a["L0_ffn_sWd"],
        cos=cos.T, sin=(sin * sign).T, rev=rev,
    )
    nc = bacc.Bacc("TRN2", target_bir_lowering=False, num_devices=1)
    arrays = {f"in_{n}": np.ascontiguousarray(v) for n, v in arrays.items()}
    args = [nc.dram_tensor(n, v.shape, mybir.dt.from_np(v.dtype), kind="ExternalInput").ap() for n, v in arrays.items()]
    out = nc.dram_tensor("out", (B, S, E), F32, kind="ExternalOutput").ap()
    block_kernel(nc, *args, out)
    r = run_bass_kernel_spmd(nc, [arrays], core_ids=[0])
    return r.results[0]["out"]
```
